# Optimizing a Trainium2 kernel written in Bass

```python
import numpy as np
import jax
import jax.numpy as jnp

def _softmax(x, axis=-1):
    return jax.nn.softmax(x, axis=axis)
def _gelu(x):
    return jax.nn.gelu(x, approximate=True)
def _silu(x):
    return jax.nn.silu(x)
def _sigmoid(x):
    return jax.nn.sigmoid(x)
def _layernorm(x, axis=-1, eps=1e-5):
    m = jnp.mean(x, axis=axis, keepdims=True)
    v = jnp.var(x, axis=axis, keepdims=True)
    return (x - m) / jnp.sqrt(v + eps)
def _scatter_add(tgt, idx, src, axis=0):
    return tgt.at[idx].add(src)
def _segment_sum(src, seg, n):
    return jax.ops.segment_sum(src, seg, n)

kernel_name = 'mk_conv_preact_d1_conv_nchw512_ecc261'

def setup_inputs(seed: int = 0):
    np.random.seed(seed)
    _w = jnp.asarray
    def _rec_inputs():
        import jax
        import jax.numpy as jnp
        _gk = jax.random.key(seed)
        x = -0.0002928 + 1 * jax.random.normal(jax.random.fold_in(_gk, 1), (2, 512, 64, 64), jnp.float32)
        return x
    x = _rec_inputs()
    def _L0_conv_setup():
        import jax, jax.numpy as jnp
        import numpy as np
        B, C, H, W = (2, 512, 64, 64)
        TC = 256

        def _w(k, o, i):
            return jax.random.normal(k, (o, i), jnp.float32) * (1.0 / np.sqrt(i))

        def _proj(x, w, g, b):
            y = jnp.einsum('oc,bcn->bon', w, x)
            return jax.nn.relu(y * g[None, :, None] + b[None, :, None])
        key = jax.random.key(seed)
        ks = jax.random.split(key, 8)
        ones = lambda n: jnp.ones((n,), jnp.float32)
        zeros = lambda n: jnp.zeros((n,), jnp.float32)
        return {'x': jax.random.normal(ks[0], (B, C, H, W), jnp.float32), 'q_w1': _w(ks[1], TC, C), 'q_g1': ones(TC), 'q_b1': zeros(TC), 'q_w2': _w(ks[2], TC, TC), 'q_g2': ones(TC), 'q_b2': zeros(TC), 'k_w1': _w(ks[3], TC, 2 * C), 'k_g1': ones(TC), 'k_b1': zeros(TC), 'k_w2': _w(ks[4], TC, TC), 'k_g2': ones(TC), 'k_b2': zeros(TC), 'v_w': _w(ks[5], TC, 2 * C), 'v_g': ones(TC), 'v_b': zeros(TC), 'o_w': _w(ks[6], C, TC), 'o_g': ones(C), 'o_b': zeros(C)}
    _L0_conv_all = _L0_conv_setup()
    _L0_conv_in = {k: v for k, v in _L0_conv_all.items() if k in ('q_w1', 'q_g1', 'q_b1', 'q_w2', 'q_g2', 'q_b2', 'k_w1', 'k_g1', 'k_b1', 'k_w2', 'k_g2', 'k_b2', 'v_w', 'v_g', 'v_b', 'o_w', 'o_g', 'o_b', )}
    del _L0_conv_all

    return {
        "x": x,
        "L0_conv_q_w1": _L0_conv_in["q_w1"],
        "L0_conv_q_g1": _L0_conv_in["q_g1"],
        "L0_conv_q_b1": _L0_conv_in["q_b1"],
        "L0_conv_q_w2": _L0_conv_in["q_w2"],
        "L0_conv_q_g2": _L0_conv_in["q_g2"],
        "L0_conv_q_b2": _L0_conv_in["q_b2"],
        "L0_conv_k_w1": _L0_conv_in["k_w1"],
        "L0_conv_k_g1": _L0_conv_in["k_g1"],
        "L0_conv_k_b1": _L0_conv_in["k_b1"],
        "L0_conv_k_w2": _L0_conv_in["k_w2"],
        "L0_conv_k_g2": _L0_conv_in["k_g2"],
        "L0_conv_k_b2": _L0_conv_in["k_b2"],
        "L0_conv_v_w": _L0_conv_in["v_w"],
        "L0_conv_v_g": _L0_conv_in["v_g"],
        "L0_conv_v_b": _L0_conv_in["v_b"],
        "L0_conv_o_w": _L0_conv_in["o_w"],
        "L0_conv_o_g": _L0_conv_in["o_g"],
        "L0_conv_o_b": _L0_conv_in["o_b"],
    }

def reference(x, L0_conv_q_w1, L0_conv_q_g1, L0_conv_q_b1, L0_conv_q_w2, L0_conv_q_g2, L0_conv_q_b2, L0_conv_k_w1, L0_conv_k_g1, L0_conv_k_b1, L0_conv_k_w2, L0_conv_k_g2, L0_conv_k_b2, L0_conv_v_w, L0_conv_v_g, L0_conv_v_b, L0_conv_o_w, L0_conv_o_g, L0_conv_o_b):
    import jax
    import jax.numpy as jnp
    def _L0_conv_ref(x, q_w1, q_g1, q_b1, q_w2, q_g2, q_b2, k_w1, k_g1, k_b1, k_w2, k_g2, k_b2, v_w, v_g, v_b, o_w, o_g, o_b):
        import jax, jax.numpy as jnp
        import numpy as np
        B, C, H, W = (2, 512, 64, 64)
        TC = 256

        def _w(k, o, i):
            return jax.random.normal(k, (o, i), jnp.float32) * (1.0 / np.sqrt(i))

        def _proj(x, w, g, b):
            y = jnp.einsum('oc,bcn->bon', w, x)
            return jax.nn.relu(y * g[None, :, None] + b[None, :, None])
        b, c, h, w = x.shape
        n = h * w
        xf = x.reshape(b, c, n)
        g_vec = jnp.mean(jax.nn.softmax(xf, axis=2) * xf, axis=2)
        g_map = jnp.broadcast_to(g_vec[:, :, None], (b, c, n))
        kv_in = jnp.concatenate([g_map, xf], axis=1)
        q = _proj(_proj(xf, q_w1, q_g1, q_b1), q_w2, q_g2, q_b2)
        k = _proj(_proj(kv_in, k_w1, k_g1, k_b1), k_w2, k_g2, k_b2)
        v = _proj(kv_in, v_w, v_g, v_b)
        tc = q.shape[1]
        sim = jnp.einsum('bcn,bcm->bnm', q, k) * tc ** (-0.5)
        attn = jax.nn.softmax(sim, axis=-1)
        ctx = jnp.einsum('bnm,bcm->bcn', attn, v)
        out = _proj(ctx, o_w, o_g, o_b)
        return out.reshape(b, -1, h, w)

    def _gn(v, G=32, eps=1e-5):
        B_, C_, H_, W_ = v.shape
        g = v.reshape(B_, G, C_ // G, H_, W_)
        m = jnp.mean(g, axis=(2, 3, 4), keepdims=True)
        s = jnp.var(g, axis=(2, 3, 4), keepdims=True)
        return ((g - m) / jnp.sqrt(s + eps)).reshape(v.shape)

    def _ln_c(v, eps=1e-6):
        m = jnp.mean(v, axis=1, keepdims=True)
        s = jnp.var(v, axis=1, keepdims=True)
        return (v - m) / jnp.sqrt(s + eps)

    def _ln_t(v, eps=1e-5):
        m = jnp.mean(v, axis=-1, keepdims=True)
        s = jnp.var(v, axis=-1, keepdims=True)
        return (v - m) / jnp.sqrt(s + eps)

    def _to_tokens(v):
        B_, C_, H_, W_ = v.shape
        return v.reshape(B_, C_, H_ * W_).transpose(0, 2, 1)
    def _from_tokens(t, like):
        B_, C_, H_, W_ = like.shape
        return t.transpose(0, 2, 1).reshape(B_, C_, H_, W_)

    x = x + _L0_conv_ref(_gn(x), L0_conv_q_w1, L0_conv_q_g1, L0_conv_q_b1, L0_conv_q_w2, L0_conv_q_g2, L0_conv_q_b2, L0_conv_k_w1, L0_conv_k_g1, L0_conv_k_b1, L0_conv_k_w2, L0_conv_k_g2, L0_conv_k_b2, L0_conv_v_w, L0_conv_v_g, L0_conv_v_b, L0_conv_o_w, L0_conv_o_g, L0_conv_o_b)
    return x


_drawn_inputs = setup_inputs


def setup_inputs(seed=0):
    import zlib

    import numpy as np

    out = dict(_drawn_inputs(seed))
    spreads = {'L0_conv_q_g1': (1.0, 0.6),
     'L0_conv_q_b1': (0.0, 0.8),
     'L0_conv_q_g2': (1.0, 0.6),
     'L0_conv_q_b2': (0.0, 0.8),
     'L0_conv_k_g1': (1.0, 0.6),
     'L0_conv_k_b1': (0.0, 0.8),
     'L0_conv_k_g2': (1.0, 0.6),
     'L0_conv_k_b2': (0.0, 0.8),
     'L0_conv_v_g': (1.0, 0.2),
     'L0_conv_v_b': (0.0, 0.421),
     'L0_conv_o_g': (1.0, 0.2),
     'L0_conv_o_b': (0.0, 0.296)}
    factors = {'L0_conv_q_w1': 8.0,
     'L0_conv_q_w2': 8.0,
     'L0_conv_k_w1': 8.0,
     'L0_conv_k_w2': 8.0,
     'L0_conv_v_w': 6.426}
    for name, (base, spread) in spreads.items():
        noise = np.random.default_rng([zlib.crc32(name.encode()), seed]).standard_normal(out[name].shape)
        drawn = base * np.exp(spread * noise) if base else spread * noise
        out[name] = jnp.asarray(drawn.astype(out[name].dtype))
    for name, factor in factors.items():
        out[name] = (out[name] * factor).astype(out[name].dtype)
    return out
```

```python
from contextlib import ExitStack

import concourse.bass as bass
from concourse import mybir

F32 = mybir.dt.float32
F32R = mybir.dt.float32r
ALU = mybir.AluOpType
ACT = mybir.ActivationFunctionType
AX = mybir.AxisListType

P = 128
BATCH, C, HW, TC = 2, 512, 4096, 256
GROUP = 16
NC = C // P
NO = TC // P
BLK = 512
NBLK = HW // BLK
TPB = BLK // P
NT = HW // P
NJ = HW // BLK
HELD = 5
CHUNK = 1024
NCH = HW // CHUNK
SCALE = float(TC) ** -0.5
EPS = 1e-5

QG1, QB1, QG2, QB2, KG1, KB1, KG2, KB2, OG, OB = 0, 2, 4, 6, 8, 10, 12, 14, 16, 20
WQ1, WK1, WV, WQ2, WK2 = 0, 4, 8, 12, 14
NW = 16

RING_LIN, RING_V, RING_S, RING_T, RING_PT, RING_CTX, RING_Y = 4, 2, 2, 2, 3, 2, 3
START = 8


def build(nc, x, w_proj, w_glob, w_out, affine, v_affine, ident_in, group_in, out):
    with ExitStack() as ctx:
        def sem(name):
            return ctx.enter_context(nc.semaphore(name))

        def sb(name, shape, dt=F32, stack=ctx):
            return stack.enter_context(nc.sbuf_tensor(name, shape, dt))

        aff = sb("aff", [P, 24])
        vaff = sb("vaff", [P, 2, TC])
        ident = sb("ident", [P, P])
        group_mean = sb("group_mean", [P, P])
        bn_part = sb("bn_part", [P, NC, 8, 6])
        mean_var = sb("mean_var", [P, NC, 2])
        mean_g = sb("mean_g", [P, NC])
        small = sb("small", [P, 6, NC])
        x_max = sb("x_max", [P, NC])
        rstd = sb("rstd", [P, NC])
        x_bias = sb("x_bias", [P, NC])
        e_bias = sb("e_bias", [P, NC])
        e_sum = sb("e_sum", [P, NC])
        ex_sum = sb("ex_sum", [P, NC])
        g_vec = sb("g_vec", [P, NC])
        k_bias = sb("k_bias", [P, NO])
        v_bias = sb("v_bias", [P, TC])
        blk_max = sb("blk_max", [P, NJ])
        neg_max = sb("neg_max", [P, 2])
        row_sums = sb("row_sums", [P, 2, NCH])
        row_sum = sb("row_sum", [P, 1])
        row_inv = sb("row_inv", [P, 2])

        with ExitStack() as region:
            x_img = sb("x_img", [P, NC, HW], stack=region)
            e_img = sb("e_img", [P, 2, HW], stack=region)
            w_raw = sb("w_raw", [P, NW, TC], stack=region)
            wg_raw = sb("wg_raw", [P, 2 * NC, TC], stack=region)
            g_wide = sb("g_wide", [P, NC, P], stack=region)
        k_hi = sb("k_hi", [P, NO, HW], F32R)
        k_lo = sb("k_lo", [P, NO, HW], F32R)
        v_hl = sb("v_hl", [P, NT, 2 * TC], F32R)

        with ExitStack() as region:
            w_hi = sb("w_hi", [P, NW, TC], F32R, region)
            w_lo = sb("w_lo", [P, NW, TC], F32R, region)
            x_blk = sb("x_blk", [P, NC, BLK], F32, region)
            x_hi = sb("x_hi", [P, NC, BLK], F32R, region)
            x_lo = sb("x_lo", [P, NC, BLK], F32R, region)
            h_hi = sb("h_hi", [P, NO, BLK], F32R, region)
            h_lo = sb("h_lo", [P, NO, BLK], F32R, region)
            lin = sb("lin", [P, RING_LIN, BLK], F32, region)
            v_tmp = sb("v_tmp", [P, TC], F32, region)
        scores = sb("scores", [P, HW])
        probs = sb("probs", [P, 2, CHUNK])
        pt_hi = sb("pt_hi", [P, RING_PT, BLK], F32R)
        pt_lo = sb("pt_lo", [P, RING_PT, BLK], F32R)
        q_raw = sb("q_raw", [P, 2, NO, P])
        q_hi = sb("q_hi", [P, 2, NO, P], F32R)
        q_lo = sb("q_lo", [P, 2, NO, P], F32R)
        ctx_part = sb("ctx_part", [P, TC])
        ctx_row = sb("ctx_row", [P, TC])
        ct_hi = sb("ct_hi", [P, NO, BLK], F32R)
        ct_lo = sb("ct_lo", [P, NO, BLK], F32R)
        wo_hi = sb("wo_hi", [P, NO, C], F32R)
        wo_lo = sb("wo_lo", [P, NO, C], F32R)
        x_res = sb("x_res", [P, 2, BLK])
        y_out = sb("y_out", [P, RING_Y, BLK])

        q_dram = nc.dram_tensor("q_scratch", (BATCH, NO, P, HW), F32, kind="Internal").ap()

        ps = ctx.enter_context(nc.psum_tensor("ps", [P, 8, BLK], F32))
        S_BANK, T_BANK, CTX_BANK, CT_BANK, O_BANK, V_BANK = 0, 2, 4, 6, 7, 4

        const_in = sem("const_in")
        x_chunk_in = [sem(f"x_chunk_in{c}") for c in range(NC)]
        w_in, wg_in, wo_in = sem("w_in"), sem("wg_in"), sem("wo_in")
        w_hi_done, w_split = sem("w_hi_done"), sem("w_split")
        wo_hi_done, wo_split = sem("wo_hi_done"), sem("wo_split")
        stat_step = sem("stat_step")
        mean_ready, var_ready = sem("mean_ready"), sem("var_ready")
        stat_mean, stat_var, ve_ready, sqrt_done = (
            sem("stat_mean"), sem("stat_var"), sem("ve_ready"), sem("sqrt_done"))
        e_bias_ready, e_done, ex_done, g_ready, glob_ready = (
            sem("e_bias_ready"), sem("e_done"), sem("ex_done"), sem("g_ready"), sem("glob_ready"))
        glob_done = sem("glob_done")
        x_in, xh_ready, xn_done, xl_ready = (
            sem("x_in"), sem("xh_ready"), sem("xn_done"), sem("xl_ready"))
        lin_ready, lin_out, h_hi_done, h_split, k_hi_done, k_split = (
            sem("lin_ready"), sem("lin_out"), sem("h_hi_done"), sem("h_split"), sem("k_hi_done"), sem("k_split"))
        v_ready, v_read, v_biased, v_hi_done, v_split = (
            sem("v_ready"), sem("v_read"), sem("v_biased"), sem("v_hi_done"), sem("v_split"))
        q_stored = sem("q_stored")
        q_in = [sem("q_in0"), sem("q_in1")]
        q_hi_done, q_split = sem("q_hi_done"), sem("q_split")
        scores_ready, scores_copied, max_ready, probs_ready = (
            sem("scores_ready"), sem("scores_copied"), sem("max_ready"), sem("probs_ready"))
        tposed, pt_hi_done, pt_split, pv_done = sem("tposed"), sem("pt_hi_done"), sem("pt_split"), sem("pv_done")
        sum_done, inv_ready, part_ready, ctx_ready = (
            sem("sum_done"), sem("inv_ready"), sem("part_ready"), sem("ctx_ready"))
        ct_ready, ct_hi_done, ct_split = sem("ct_ready"), sem("ct_hi_done"), sem("ct_split")
        o_ready, o_relu, y_ready = sem("o_ready"), sem("o_relu"), sem("y_ready")
        x_res_in = [sem("x_res_in0"), sem("x_res_in1")]
        y_stored = [sem(f"y_stored{s}") for s in range(RING_Y)]

        slot_stores = [len(range(s, NC, RING_Y)) for s in range(RING_Y)]

        block = ctx.enter_context(nc.Block())

        def key_cols(j):
            return slice(j * BLK, (j + 1) * BLK)

        @block.gpsimd
        def _(pool):
            for s in (lin_out, k_split, v_read, v_split, scores_ready, scores_copied, max_ready, probs_ready, tposed,
                      pt_split, pv_done, inv_ready, part_ready, ctx_ready, ct_ready, ct_split, o_ready, o_relu,
                      *y_stored):
                pool.sem_inc(s, START)

            def add_residual(g, co):
                pool.wait_ge(o_relu, START + g * NC + co + 1)
                pool.wait_ge(x_res_in[co % 2], g * (16 * NC // 2) + 16 * (co // 2) + 16)
                nc.gpsimd.tensor_tensor(y_out[:, co % RING_Y], y_out[:, co % RING_Y], x_res[:, co % 2], ALU.add)\
                    .then_inc(y_ready, 1)

            with pool.Fori(0, BATCH) as b:
                with pool.Fori(0, NBLK) as blk:
                    for co in range(NC):
                        add_residual(b * NBLK + blk, co)

        @block.sync
        def _(sp):
            sp.dma_start(aff[:], affine).then_inc(const_in, 16)
            sp.dma_start(vaff[:], v_affine).then_inc(const_in, 16)
            sp.dma_start(ident[:], ident_in).then_inc(const_in, 16)
            sp.dma_start(group_mean[:], group_in).then_inc(const_in, 16)

            def load_x(b, blk):
                sp.dma_start(x_blk[:], x[bass.ds(b, 1), :, :, bass.ds(blk * BLK, BLK)]
                             .rearrange("b c p n -> p (b c) n")).then_inc(x_in, 16)

            def store_q(b, blk, first, oc):
                sp.wait_ge(lin_out, START + first + 2 + oc + 1)
                sp.dma_start(q_dram[bass.ds(b, 1), oc, :, bass.ds(blk * BLK, BLK)]
                             .rearrange("b p n -> p (b n)"), lin[:, 2 + oc, :]).then_inc(q_stored, 16)

            def load_q(b, tile, slot):
                sp.dma_start(q_raw[:, slot], q_dram[bass.ds(b, 1), :, :, bass.ds(tile * P, P)]
                             .rearrange("b o p n -> p (b o) n")).then_inc(q_in[slot], 16)

            def load_res(b, blk, co):
                sp.dma_start(x_res[:, co % 2], x[bass.ds(b, 1), co, :, bass.ds(blk * BLK, BLK)]
                             .rearrange("b p n -> p (b n)")).then_inc(x_res_in[co % 2], 16)

            def attend(b, blk, last):
                t0 = (b * NBLK + blk) * TPB
                y0 = (b * NBLK + blk) * NC
                sp.wait_ge(wo_split, b + 1)
                load_res(b, blk, 0)
                load_res(b, blk, 1)
                for i in range(TPB):
                    if not last or i < TPB - 2:
                        sp.wait_ge(q_split, t0 + i + 1)
                        load_q(b, blk * TPB + i + 2, i % 2)
                for co in range(NC):
                    sp.wait_ge(y_ready, y0 + co + 1)
                    sp.dma_start(out[bass.ds(b, 1), co, :, bass.ds(blk * BLK, BLK)]
                                 .rearrange("b p n -> p (b n)"), y_out[:, co % RING_Y]).then_inc(y_stored[co % RING_Y], 16)
                    if co + 2 < NC:
                        load_res(b, blk, co + 2)

            with sp.Fori(0, BATCH) as b:
                for s in range(RING_Y):
                    sp.wait_ge(y_stored[s], START + b * (16 * NBLK * slot_stores[s]))
                for c in range(NC):
                    sp.dma_start(x_img[:, c], x[bass.ds(b, 1), c].rearrange("b p n -> p (b n)"))\
                        .then_inc(x_chunk_in[c], 16)
                sp.dma_start(w_raw[:], w_proj.rearrange("(r p) o -> p r o", p=P)).then_inc(w_in, 16)
                sp.dma_start(wg_raw[:], w_glob.rearrange("(r p) o -> p r o", p=P)).then_inc(wg_in, 16)
                load_x(b, 0)
                with sp.Fori(0, NBLK - 1) as blk:
                    g = b * NBLK + blk
                    sp.wait_ge(xl_ready, g * NC + NC)
                    load_x(b, blk + 1)
                    for oc in range(NO):
                        store_q(b, blk, g * 8, oc)
                for oc in range(NO):
                    store_q(b, NBLK - 1, b * (8 * NBLK) + 8 * (NBLK - 1), oc)
                sp.wait_ge(q_stored, b * (16 * NO * NBLK) + 16 * NO * NBLK)
                sp.wait_ge(v_split, START + b * NT + NT)
                sp.wait_ge(k_split, START + b * (NO * NBLK) + NO * NBLK)
                sp.dma_start(x_res[:], w_out.rearrange("(r p) o -> p r o", p=P)).then_inc(wo_in, 16)
                load_q(b, 0, 0)
                load_q(b, 1, 1)
                with sp.Fori(0, NBLK - 1) as blk:
                    attend(b, blk, False)
                attend(b, NBLK - 1, True)
            for s in range(RING_Y):
                sp.wait_ge(y_stored[s], START + BATCH * 16 * NBLK * slot_stores[s])
            sp.wait_ge(q_stored, BATCH * 16 * NO * NBLK)

        @block.scalar
        def _(act):
            def split_x(g, first):
                act.wait_ge(x_in, g * 16 + 16)
                if not first:
                    act.wait_ge(v_ready, g * TPB)
                for c in range(NC):
                    nc.scalar.activation(x_hi[:, c], x_blk[:, c], ACT.Identity, bias=x_bias[:, c:c + 1],
                                         scale=rstd[:, c:c + 1]).then_inc(xh_ready, 1)

            def relu(g, n, gain, bias):
                act.wait_ge(lin_ready, g * 8 + n + 1)
                if n in (2, 3):
                    act.wait_ge(k_split, START + g * NO)
                if n == 6:
                    act.wait_ge(q_stored, g * (16 * NO) + 16 * NO)
                nc.scalar.activation(lin[:, n % RING_LIN], ps[:, n % RING_LIN], ACT.Relu, bias=bias,
                                     scale=gain).then_inc(lin_out, 1)

            def project(g, last):
                relu(g, 0, aff[:, QG1:QG1 + 1], aff[:, QB1:QB1 + 1])
                relu(g, 1, aff[:, QG1 + 1:QG1 + 2], aff[:, QB1 + 1:QB1 + 2])
                relu(g, 2, aff[:, QG2:QG2 + 1], aff[:, QB2:QB2 + 1])
                relu(g, 3, aff[:, QG2 + 1:QG2 + 2], aff[:, QB2 + 1:QB2 + 2])
                relu(g, 4, aff[:, KG1:KG1 + 1], k_bias[:, 0:1])
                relu(g, 5, aff[:, KG1 + 1:KG1 + 2], k_bias[:, 1:2])
                if not last:
                    split_x(g + 1, False)
                relu(g, 6, aff[:, KG2:KG2 + 1], aff[:, KB2:KB2 + 1])
                relu(g, 7, aff[:, KG2 + 1:KG2 + 2], aff[:, KB2 + 1:KB2 + 2])

            def q_high(slot, pair, scored):
                act.wait_ge(q_in[slot], pair * 16 + 16)
                act.wait_ge(scores_ready, START + scored)
                nc.scalar.copy(q_hi[:, slot], q_raw[:, slot]).then_inc(q_hi_done, 1)

            def exponential(t, parity, c):
                if c == 0:
                    act.wait_ge(max_ready, START + t + 1)
                    act.wait_ge(inv_ready, START + t - 1)
                act.wait_ge(tposed, START + t * (2 * NCH) + 2 * c - 2)
                nc.scalar.activation(probs[:, c % 2], scores[:, c * CHUNK:(c + 1) * CHUNK], ACT.Exp,
                                     bias=neg_max[:, parity:parity + 1],
                                     accum_out=row_sums[:, parity, c:c + 1]).then_inc(probs_ready, 1)

            def pt_high(t, j):
                act.wait_ge(tposed, START + t * NJ + j + 1)
                act.wait_ge(pv_done, START + t * NJ + j + 1 - (2 if j < 2 else RING_PT))
                nc.scalar.copy(pt_hi[:, j % RING_PT], ps[:, T_BANK + j % RING_T]).then_inc(pt_hi_done, 1)

            def ctx_part_out(t, parity):
                act.wait_ge(pv_done, START + t * NJ + NJ)
                act.wait_ge(inv_ready, START + t + 1)
                act.wait_ge(ctx_ready, START + t)
                nc.scalar.activation(ctx_part[:], ps[:, CTX_BANK + parity, TC:2 * TC], ACT.Copy,
                                     scale=row_inv[:, parity:parity + 1]).then_inc(part_ready, 1)

            def ct_high(t, y0, i):
                act.wait_ge(ct_ready, START + t + 1)
                if i == 0:
                    act.wait_ge(o_ready, START + y0)
                nc.scalar.copy(ct_hi[:, :, i * P:(i + 1) * P], ps[:, CT_BANK, 0:TC].rearrange("p (o n) -> p o n", o=NO))\
                    .then_inc(ct_hi_done, 1)

            def project_out(g, co):
                act.wait_ge(o_ready, START + g * NC + co + 1)
                act.wait_ge(y_stored[co % RING_Y], START + g * (16 * slot_stores[co % RING_Y])
                            + 16 * (co // RING_Y))
                nc.scalar.activation(y_out[:, co % RING_Y], ps[:, O_BANK - co % 2], ACT.Relu,
                                     bias=aff[:, OB + co:OB + co + 1], scale=aff[:, OG + co:OG + co + 1])\
                    .then_inc(o_relu, 1)

            def attend(b, blk, last):
                g = b * NBLK + blk
                for i in range(TPB):
                    t = g * TPB + i
                    more = not last or i < TPB - 1
                    for j in range(NJ):
                        pt_high(t, j)
                        if j in (1, 3):
                            exponential(t, i % 2, 2 + j // 2)
                        if i > 0 and j == 2:
                            ctx_part_out(t - 1, (i - 1) % 2)
                        if i > 0 and j == 4:
                            ct_high(t - 1, g * NC, i - 1)
                        if j == 5 and (not last or i < TPB - 2):
                            q_high(i % 2, g * (TPB // 2) + i // 2 + 1, t * NJ + NJ)
                    if i == TPB - 1:
                        ctx_part_out(t, i % 2)
                        ct_high(t, g * NC, i)
                    if i == TPB - 1:
                        project_out(g, 0)
                        project_out(g, 1)
                    if more:
                        exponential(t + 1, (i + 1) % 2, 0)
                        exponential(t + 1, (i + 1) % 2, 1)
                for co in range(2, NC):
                    project_out(g, co)

            act.wait_ge(const_in, 64)
            with act.Fori(0, BATCH) as b:
                act.wait_ge(w_in, b * 16 + 16)
                nc.scalar.copy(w_hi[:], w_raw[:]).then_inc(w_hi_done, 1)
                act.wait_ge(ve_ready, b + 1)
                nc.scalar.activation(small[:, 1], small[:, 0], ACT.Sqrt).then_inc(sqrt_done, 1)
                act.wait_ge(e_bias_ready, b + 1)
                for c in range(NC):
                    if c >= 2:
                        act.wait_ge(ex_done, b * NC + c - 1)
                    nc.scalar.activation(e_img[:, c % 2], x_img[:, c], ACT.Exp, bias=e_bias[:, c:c + 1],
                                         scale=rstd[:, c:c + 1], accum_out=e_sum[:, c:c + 1]).then_inc(e_done, 1)
                act.wait_ge(glob_done, b + 1)
                split_x(b * NBLK, True)
                with act.Fori(0, NBLK - 1) as blk:
                    project(b * NBLK + blk, False)
                project(b * NBLK + (NBLK - 1), True)
                q_high(0, b * (NT // 2), b * (NJ * NT))
                q_high(1, b * (NT // 2), b * (NJ * NT))
                act.wait_ge(wo_in, b * 16 + 16)
                nc.scalar.copy(wo_hi[:], x_res[:]).then_inc(wo_hi_done, 1)
                exponential(b * NT, 0, 0)
                exponential(b * NT, 0, 1)
                with act.Fori(0, NBLK - 1) as blk:
                    attend(b, blk, False)
                attend(b, NBLK - 1, True)

        @block.tensor
        def _(pe):
            def three(out_ap, terms, done):
                n = len(terms)
                for k, (w, m) in enumerate(terms):
                    last = nc.tensor.matmul(out_ap, w, m, start=(k == 0), stop=(k == n - 1))
                last.then_inc(done, 1)

            def linear(g, n, row, chunks, oc, hi, lo):
                pe.wait_ge(lin_out, START + g * 8 + n + 1 - RING_LIN)
                cols = slice(oc * P, (oc + 1) * P)
                terms = []
                for c in range(chunks):
                    terms += [(w_hi[:, row + c, cols], hi[:, c]), (w_lo[:, row + c, cols], hi[:, c]),
                              (w_hi[:, row + c, cols], lo[:, c])]
                three(ps[:, n % RING_LIN], terms, lin_ready)

            def values(g, u):
                pe.wait_ge(v_read, START + g * TPB + u + 1 - RING_V)
                cols = slice(u * P, (u + 1) * P)
                terms = []
                for c in range(NC):
                    terms += [(x_hi[:, c, cols], w_hi[:, WV + c]), (x_hi[:, c, cols], w_lo[:, WV + c]),
                              (x_lo[:, c, cols], w_hi[:, WV + c])]
                three(ps[:, V_BANK + u % RING_V, 0:TC], terms, v_ready)

            def score(t, slot, j):
                pe.wait_ge(scores_copied, START + t * NJ + j + 1 - RING_S)
                terms = []
                for c in range(NO):
                    terms += [(q_hi[:, slot, c], k_hi[:, c, key_cols(j)]), (q_hi[:, slot, c], k_lo[:, c, key_cols(j)]),
                              (q_lo[:, slot, c], k_hi[:, c, key_cols(j)])]
                three(ps[:, S_BANK + j % RING_S], terms, scores_ready)

            def turn(t, j):
                if j % 2 == 0:
                    pe.wait_ge(probs_ready, START + t * NCH + j // 2 + 1)
                pe.wait_ge(pt_split, START + t * NJ + j + 1 - RING_T)
                for k in range(BLK // P):
                    at = (j % 2) * BLK + k * P
                    last = nc.tensor.transpose(ps[:, T_BANK + j % RING_T, k * P:(k + 1) * P],
                                               probs[:, (j // 2) % 2, at:at + P], ident[:])
                last.then_inc(tposed, 1)

            def context(t, parity, j):
                if j == 0:
                    pe.wait_ge(ctx_ready, START + t + 1 - RING_CTX)
                pe.wait_ge(pt_split, START + t * NJ + j + 1)
                bank = ps[:, CTX_BANK + parity]
                for k in range(BLK // P):
                    m = j * (BLK // P) + k
                    cols = slice(k * P, (k + 1) * P)
                    nc.tensor.matmul(bank, pt_hi[:, j % RING_PT, cols], v_hl[:, m], start=(m == 0), stop=False)
                    last = nc.tensor.matmul(bank[:, 0:TC], pt_lo[:, j % RING_PT, cols], v_hl[:, m, 0:TC],
                                            start=False, stop=(m == NT - 1))
                last.then_inc(pv_done, 1)

            def turn_context(t, y0, i):
                pe.wait_ge(ctx_ready, START + t + 1)
                pe.wait_ge(ct_split, START + t)
                if i == 0:
                    pe.wait_ge(o_relu, START + y0)
                for c in range(NO):
                    last = nc.tensor.transpose(ps[:, CT_BANK, c * P:(c + 1) * P], ctx_row[:, c * P:(c + 1) * P], ident[:])
                last.then_inc(ct_ready, 1)

            def project_out(g, co):
                if co == 0:
                    pe.wait_ge(ct_split, START + g * TPB + TPB)
                pe.wait_ge(o_relu, START + g * NC + (co - 1 if co >= 2 else 0))
                cols = slice(co * P, (co + 1) * P)
                terms = []
                for c in range(NO):
                    terms += [(wo_hi[:, c, cols], ct_hi[:, c]), (wo_lo[:, c, cols], ct_hi[:, c]),
                              (wo_hi[:, c, cols], ct_lo[:, c])]
                three(ps[:, O_BANK - co % 2], terms, o_ready)

            def attend(b, blk, last):
                g = b * NBLK + blk
                for i in range(TPB):
                    t = g * TPB + i
                    more = not last or i < TPB - 1
                    own = i == TPB - 1
                    if more:
                        pe.wait_ge(q_split, t + 2)
                    for j in range(NJ - 1):
                        if more and not (own and j >= HELD):
                            score(t + 1, (i + 1) % 2, j)
                        turn(t, j)
                        if own and j == NJ - 2:
                            turn(t, NJ - 1)
                        if j > 0:
                            context(t, i % 2, j - 1)
                        if i > 0 and j == 3:
                            turn_context(t - 1, g * NC, i - 1)
                    if not own:
                        turn(t, NJ - 1)
                        if more:
                            score(t + 1, (i + 1) % 2, NJ - 1)
                    context(t, i % 2, NJ - 2)
                    context(t, i % 2, NJ - 1)
                    if own:
                        if more:
                            score(t + 1, (i + 1) % 2, HELD)
                        turn_context(t, g * NC, i)
                        if more:
                            for j in range(HELD + 1, NJ):
                                score(t + 1, (i + 1) % 2, j)
                        for co in range(NC):
                            project_out(g, co)

            pe.wait_ge(const_in, 64)
            with pe.Fori(0, BATCH) as b:
                pe.wait_ge(stat_mean, b + 1)
                nc.tensor.matmul(ps[:, 7, 0:NC], group_mean[:], small[:, 2], start=True, stop=True)\
                    .then_inc(mean_ready, 1)
                pe.wait_ge(stat_var, b + 1)
                nc.tensor.matmul(ps[:, 7, 0:NC], group_mean[:], small[:, 3], start=True, stop=True)\
                    .then_inc(var_ready, 1)
                pe.wait_ge(g_ready, b + 1)
                pe.wait_ge(wg_in, b * 16 + 16)
                for oc in range(NO):
                    for c in range(NC):
                        nc.tensor.matmul(ps[:, 7, 8 + oc:9 + oc], wg_raw[:, c, oc * P:(oc + 1) * P], g_vec[:, c:c + 1],
                                         start=(c == 0), stop=(c == NC - 1))
                for c in range(NC):
                    last = nc.tensor.matmul(ps[:, 6, 0:TC], g_wide[:, c], wg_raw[:, NC + c], start=(c == 0),
                                            stop=(c == NC - 1))
                last.then_inc(glob_ready, 1)
                with pe.Fori(0, NBLK) as blk:
                    g = b * NBLK + blk
                    pe.wait_ge(w_split, b + 1)
                    pe.wait_ge(xl_ready, g * NC + NC)
                    linear(g, 0, WQ1, NC, 0, x_hi, x_lo)
                    linear(g, 1, WQ1, NC, 1, x_hi, x_lo)
                    values(g, 0)
                    values(g, 1)
                    pe.wait_ge(h_split, g * 4 + 2)
                    linear(g, 2, WQ2, NO, 0, h_hi, h_lo)
                    linear(g, 3, WQ2, NO, 1, h_hi, h_lo)
                    linear(g, 4, WK1, NC, 0, x_hi, x_lo)
                    linear(g, 5, WK1, NC, 1, x_hi, x_lo)
                    values(g, 2)
                    values(g, 3)
                    pe.wait_ge(h_split, g * 4 + 4)
                    linear(g, 6, WK2, NO, 0, h_hi, h_lo)
                    linear(g, 7, WK2, NO, 1, h_hi, h_lo)
                pe.wait_ge(q_split, b * NT + 1)
                pe.wait_ge(wo_split, b + 1)
                for j in range(NJ):
                    score(b * NT, 0, j)
                with pe.Fori(0, NBLK - 1) as blk:
                    attend(b, blk, False)
                attend(b, NBLK - 1, True)

        @block.vector
        def _(dve):
            STEPS = 21

            def split_x(g):
                for c in range(NC):
                    dve.wait_ge(xh_ready, g * NC + c + 1)
                    nc.vector.tensor_scalar(x_blk[:, c], x_blk[:, c], rstd[:, c:c + 1], x_bias[:, c:c + 1],
                                            ALU.mult, ALU.add).then_inc(xn_done, 1)
                    dve.wait_ge(xn_done, g * NC + c + 1)
                    nc.vector.tensor_tensor(x_lo[:, c], x_blk[:, c], x_hi[:, c].bitcast(F32), ALU.subtract)\
                        .then_inc(xl_ready, 1)

            def split_h(g, n, oc, m):
                dve.wait_ge(lin_out, START + g * 8 + n + 1)
                nc.vector.tensor_copy(h_hi[:, oc], lin[:, n % RING_LIN]).then_inc(h_hi_done, 1)
                dve.wait_ge(h_hi_done, g * 4 + m + 1)
                nc.vector.tensor_tensor(h_lo[:, oc], lin[:, n % RING_LIN], h_hi[:, oc].bitcast(F32), ALU.subtract)\
                    .then_inc(h_split, 1)

            def split_k(g, blk, oc):
                cols = bass.ds(blk * BLK, BLK)
                dve.wait_ge(lin_out, START + g * 8 + 6 + oc + 1)
                nc.vector.tensor_copy(k_hi[:, oc, cols], lin[:, 2 + oc]).then_inc(k_hi_done, 1)
                dve.wait_ge(k_hi_done, g * NO + oc + 1)
                nc.vector.tensor_tensor(k_lo[:, oc, cols], lin[:, 2 + oc], k_hi[:, oc, cols].bitcast(F32),
                                        ALU.subtract).then_inc(k_split, 1)

            def split_v(g, blk, u):
                n = g * TPB + u
                dve.wait_ge(v_ready, n + 1)
                dve.wait_ge(v_split, START + n)
                nc.vector.tensor_tensor(v_tmp[:], ps[:, V_BANK + u % RING_V, 0:TC], vaff[:, 0], ALU.mult)\
                    .then_inc(v_read, 1)
                dve.wait_ge(v_read, START + n + 1)
                nc.vector.tensor_tensor(v_tmp[:], v_tmp[:], v_bias[:], ALU.add).then_inc(v_biased, 1)
                dve.wait_ge(v_biased, n + 1)
                m = blk * TPB + u
                hi = v_hl[:, bass.ds(m, 1), 0:TC].rearrange("p a c -> p (a c)")
                lo = v_hl[:, bass.ds(m, 1), TC:2 * TC].rearrange("p a c -> p (a c)")
                nc.vector.tensor_scalar(hi, v_tmp[:], 0.0, None, ALU.max).then_inc(v_hi_done, 1)
                dve.wait_ge(v_hi_done, n + 1)
                nc.vector.scalar_tensor_tensor(out=lo, in0=v_tmp[:], scalar=0.0, in1=hi.bitcast(F32), op0=ALU.max,
                                               op1=ALU.subtract).then_inc(v_split, 1)

            def project(b, blk, last):
                g = b * NBLK + blk
                split_h(g, 0, 0, 0)
                split_h(g, 1, 1, 1)
                split_v(g, blk, 0)
                split_v(g, blk, 1)
                split_h(g, 4, 0, 2)
                split_h(g, 5, 1, 3)
                split_v(g, blk, 2)
                if not last:
                    split_x(g + 1)
                split_v(g, blk, 3)
                split_k(g, blk, 0)
                split_k(g, blk, 1)

            def copy_scores(t, j):
                if j % 2 == 0:
                    dve.wait_ge(probs_ready, START + (t - 1) * NCH + j // 2 + 1)
                if j == 0:
                    dve.wait_ge(max_ready, START + t)
                dve.wait_ge(scores_ready, START + t * NJ + j + 1)
                nc.vector.tensor_scalar(scores[:, key_cols(j)], ps[:, S_BANK + j % RING_S], SCALE, None, ALU.mult,
                                        ALU.max, accum_out=blk_max[:, j:j + 1]).then_inc(scores_copied, 1)

            def row_max(t, parity):
                dve.wait_ge(scores_copied, START + t * NJ + NJ)
                nc.vector.tensor_reduce(neg_max[:, parity:parity + 1], blk_max[:], AX.X, ALU.max, negate=True)\
                    .then_inc(max_ready, 1)

            def pt_low(t, j):
                dve.wait_ge(pt_hi_done, t * NJ + j + 1)
                nc.vector.tensor_tensor(pt_lo[:, j % RING_PT], ps[:, T_BANK + j % RING_T],
                                        pt_hi[:, j % RING_PT].bitcast(F32), ALU.subtract).then_inc(pt_split, 1)

            def row_inverse(t, parity):
                dve.wait_ge(probs_ready, START + t * NCH + NCH)
                dve.wait_ge(inv_ready, START + t)
                nc.vector.tensor_reduce(row_sum[:], row_sums[:, parity], AX.X, ALU.add).then_inc(sum_done, 1)
                dve.wait_ge(sum_done, t + 1)
                dve.wait_ge(part_ready, START + t - 1)
                nc.vector.reciprocal(row_inv[:, parity:parity + 1], row_sum[:]).then_inc(inv_ready, 1)

            def finish_context(t, parity):
                dve.wait_ge(part_ready, START + t + 1)
                dve.wait_ge(ct_ready, START + t)
                nc.vector.scalar_tensor_tensor(out=ctx_row[:], in0=ps[:, CTX_BANK + parity, 0:TC],
                                               scalar=row_inv[:, parity:parity + 1], in1=ctx_part[:],
                                               op0=ALU.mult, op1=ALU.add).then_inc(ctx_ready, 1)

            def ct_low(t, i):
                dve.wait_ge(ct_hi_done, t + 1)
                nc.vector.tensor_tensor(ct_lo[:, :, i * P:(i + 1) * P],
                                        ps[:, CT_BANK, 0:TC].rearrange("p (o n) -> p o n", o=NO),
                                        ct_hi[:, :, i * P:(i + 1) * P].bitcast(F32), ALU.subtract).then_inc(ct_split, 1)

            def q_low(t, slot):
                dve.wait_ge(q_hi_done, t + 1)
                nc.vector.tensor_tensor(q_lo[:, slot], q_raw[:, slot], q_hi[:, slot].bitcast(F32), ALU.subtract)\
                    .then_inc(q_split, 1)

            def attend(b, blk, last):
                g = b * NBLK + blk
                for i in range(TPB):
                    t = g * TPB + i
                    more = not last or i < TPB - 1
                    own = i == TPB - 1
                    for j in range(NJ):
                        if more and j < (HELD if own else NJ - 1):
                            copy_scores(t + 1, j)
                        pt_low(t, j)
                        if more and not own and j == NJ - 1:
                            copy_scores(t + 1, j)
                            row_max(t + 1, (i + 1) % 2)
                        if i > 0 and j == 2:
                            finish_context(t - 1, (i - 1) % 2)
                        if i > 0 and j == 4:
                            ct_low(t - 1, i - 1)
                        if j == 4:
                            row_inverse(t, i % 2)
                        if j == 5 and (not last or i < TPB - 2):
                            q_low(t + 2, i % 2)
                    if own:
                        finish_context(t, i % 2)
                        if more:
                            copy_scores(t + 1, HELD)
                        ct_low(t, i)
                        if more:
                            for j in range(HELD + 1, NJ):
                                copy_scores(t + 1, j)
                            row_max(t + 1, (i + 1) % 2)

            dve.wait_ge(const_in, 64)
            with dve.Fori(0, BATCH) as b:
                done = [0]

                def link(ins):
                    done[0] += 1
                    ins.then_inc(stat_step, 1)
                    dve.wait_ge(stat_step, b * STEPS + done[0])

                for c in range(NC):
                    dve.wait_ge(x_chunk_in[c], b * 16 + 16)
                    for j in range(8):
                        last = nc.vector.bn_stats(bn_part[:, c, j], x_img[:, c, key_cols(j)])
                    link(last)
                    nc.vector.tensor_reduce(x_max[:, c:c + 1], x_img[:, c], AX.X, ALU.max)
                    link(nc.vector.bn_aggr(mean_var[:, c], bn_part[:, c]))
                nc.vector.tensor_copy(small[:, 2], mean_var[:, :, 0]).then_inc(stat_mean, 1)
                dve.wait_ge(w_hi_done, b + 1)
                nc.vector.tensor_tensor(w_lo[:], w_raw[:], w_hi[:].bitcast(F32), ALU.subtract).then_inc(w_split, 1)
                dve.wait_ge(mean_ready, b + 1)
                link(nc.vector.tensor_copy(mean_g[:], ps[:, 7, 0:NC]))
                link(nc.vector.tensor_tensor(small[:, 4], mean_var[:, :, 0], mean_g[:], ALU.subtract))
                link(nc.vector.tensor_tensor(small[:, 4], small[:, 4], small[:, 4], ALU.mult))
                nc.vector.tensor_tensor(small[:, 3], small[:, 4], mean_var[:, :, 1], ALU.add).then_inc(stat_var, 1)
                dve.wait_ge(var_ready, b + 1)
                nc.vector.tensor_scalar(small[:, 0], ps[:, 7, 0:NC], EPS, None, ALU.add).then_inc(ve_ready, 1)
                dve.wait_ge(sqrt_done, b + 1)
                link(nc.vector.reciprocal(small[:, 4], small[:, 1]))
                link(nc.vector.tensor_tensor(small[:, 5], small[:, 4], small[:, 4], ALU.mult))
                link(nc.vector.tensor_tensor(small[:, 5], small[:, 5], small[:, 0], ALU.mult))
                link(nc.vector.tensor_scalar(small[:, 5], small[:, 5], -0.5, 1.5, ALU.mult, ALU.add))
                link(nc.vector.tensor_tensor(rstd[:], small[:, 4], small[:, 5], ALU.mult))
                nc.vector.scalar_tensor_tensor(out=x_bias[:], in0=mean_g[:], scalar=-1.0, in1=rstd[:], op0=ALU.mult,
                                               op1=ALU.mult)
                nc.vector.scalar_tensor_tensor(out=e_bias[:], in0=x_max[:], scalar=-1.0, in1=rstd[:], op0=ALU.mult,
                                               op1=ALU.mult).then_inc(e_bias_ready, 1)
                for c in range(NC):
                    dve.wait_ge(e_done, b * NC + c + 1)
                    nc.vector.tensor_tensor_reduce(e_img[:, c % 2], e_img[:, c % 2], x_img[:, c], 1.0, 0.0, ALU.mult,
                                                   ALU.add, ex_sum[:, c:c + 1]).then_inc(ex_done, 1)
                dve.wait_ge(ex_done, b * NC + NC)
                link(nc.vector.reciprocal(small[:, 4], e_sum[:]))
                link(nc.vector.tensor_tensor(small[:, 4], small[:, 4], ex_sum[:], ALU.mult))
                link(nc.vector.tensor_tensor(small[:, 4], small[:, 4], mean_g[:], ALU.subtract))
                link(nc.vector.scalar_tensor_tensor(out=g_vec[:], in0=small[:, 4], scalar=1.0 / HW, in1=rstd[:],
                                                    op0=ALU.mult, op1=ALU.mult))
                for c in range(NC):
                    last = nc.vector.tensor_scalar(g_wide[:, c], group_mean[:], 0.0, g_vec[:, c:c + 1], ALU.mult, ALU.add)
                last.then_inc(g_ready, 1)
                dve.wait_ge(glob_ready, b + 1)
                nc.vector.tensor_tensor(k_bias[:], ps[:, 7, 8:8 + NO], aff[:, KG1:KG1 + NO], ALU.mult)
                link(nc.vector.tensor_tensor(v_bias[:], ps[:, 6, 0:TC], vaff[:, 0], ALU.mult))
                nc.vector.tensor_tensor(k_bias[:], k_bias[:], aff[:, KB1:KB1 + NO], ALU.add)
                nc.vector.tensor_tensor(v_bias[:], v_bias[:], vaff[:, 1], ALU.add).then_inc(glob_done, 1)
                assert done[0] <= STEPS, done[0]
                for _ in range(STEPS - done[0]):
                    dve.sem_inc(stat_step, 1)
                dve.wait_ge(glob_done, b + 1)
                split_x(b * NBLK)
                with dve.Fori(0, NBLK - 1) as blk:
                    project(b, blk, False)
                project(b, NBLK - 1, True)
                q_low(b * NT, 0)
                q_low(b * NT + 1, 1)
                dve.wait_ge(wo_hi_done, b + 1)
                nc.vector.tensor_tensor(wo_lo[:], x_res[:], wo_hi[:].bitcast(F32), ALU.subtract).then_inc(wo_split, 1)
                for j in range(NJ):
                    copy_scores(b * NT, j)
                row_max(b * NT, 0)
                with dve.Fori(0, NBLK - 1) as blk:
                    attend(b, blk, False)
                attend(b, NBLK - 1, True)


def kernel(**inputs):
    import numpy as np
    import concourse.bacc as bacc
    from concourse.bass_utils import run_bass_kernel_spmd as run

    a = {k.replace("L0_conv_", ""): np.asarray(v) for k, v in inputs.items()}

    def per_channel(v):
        return v.reshape(-1, P).T

    k_t, v_t = a["k_w1"].T, a["v_w"].T
    w_proj = np.concatenate([a["q_w1"].T, k_t[C:], v_t[C:], a["q_w2"].T, a["k_w2"].T], 0)
    w_glob = np.concatenate([k_t[:C], v_t[:C]], 0)
    affine = np.concatenate([per_channel(a[n]) for n in
                             ("q_g1", "q_b1", "q_g2", "q_b2", "k_g1", "k_b1", "k_g2", "k_b2", "o_g", "o_b")], 1)
    v_affine = np.stack([np.repeat(a["v_g"][None], P, 0), np.repeat(a["v_b"][None], P, 0)], 1)
    channel = np.arange(P)
    same_group = channel[:, None] // GROUP == channel[None] // GROUP
    arrays = {
        "x": a["x"].reshape(BATCH, NC, P, HW),
        "w_proj": w_proj,
        "w_glob": w_glob,
        "w_out": a["o_w"].T,
        "affine": affine,
        "v_affine": v_affine,
        "ident": np.eye(P, dtype=np.float32),
        "group": np.where(same_group, 1.0 / GROUP, 0.0).astype(np.float32),
    }
    arrays = {f"in_{k}_dram": np.ascontiguousarray(v) for k, v in arrays.items()}
    nc = bacc.Bacc("TRN2", target_bir_lowering=False, num_devices=1)
    args = [nc.dram_tensor(k, v.shape, F32, kind="ExternalInput").ap() for k, v in arrays.items()]
    out = nc.dram_tensor("out_0_dram", (BATCH, NC, P, HW), F32, kind="ExternalOutput").ap()
    build(nc, *args, out)
    r = run(nc, [arrays], core_ids=[0])
    return r.results[0]["out_0_dram"].reshape(BATCH, C, 64, 64)
```

```python
from contextlib import ExitStack

import concourse.bass as bass
from concourse import mybir

F32 = mybir.dt.float32
F32R = mybir.dt.float32r
ALU = mybir.AluOpType
ACT = mybir.ActivationFunctionType
AX = mybir.AxisListType

P = 128
BATCH, C, HW, TC = 2, 512, 4096, 256
GROUP = 16
NC = C // P
NO = TC // P
BLK = 512
NBLK = HW // BLK
TPB = BLK // P
NT = HW // P
NJ = HW // BLK
HELD = 5
CHUNK = 1024
NCH = HW // CHUNK
PAIR = 2 * BLK
NPAIR = HW // PAIR
HALF = BLK // 2
W_COLS = TC // NPAIR
Q_STEPS = NBLK + 1
SCALE = float(TC) ** -0.5
EPS = 1e-5

QG1, QB1, QG2, QB2, KG1, KB1, KG2, KB2, OG, OB = 0, 2, 4, 6, 8, 10, 12, 14, 16, 20
WQ1, WQ2, WK1, WV, WK2 = 0, 4, 6, 10, 14
NW = 16

RING_V, RING_S, RING_T, RING_PT, RING_CTX, RING_Y = 2, 2, 2, 3, 2, 3
START = 8


def build(nc, x, w_proj, w_glob, w_out, affine, v_affine, ident_in, group_in, out):
    with ExitStack() as ctx:
        def sem(name):
            return ctx.enter_context(nc.semaphore(name))

        def sb(name, shape, dt=F32, stack=ctx):
            return stack.enter_context(nc.sbuf_tensor(name, shape, dt))

        aff = sb("aff", [P, 24])
        vaff = sb("vaff", [P, 2, TC])
        ident = sb("ident", [P, P])
        group_mean = sb("group_mean", [P, P])
        bn_part = sb("bn_part", [P, NC, NBLK, 6])
        max_part = sb("max_part", [P, NC, NBLK])
        mean_var = sb("mean_var", [P, NC, 2])
        mean_g = sb("mean_g", [P, NC])
        small = sb("small", [P, 6, NC])
        x_max = sb("x_max", [P, NC])
        rstd = sb("rstd", [P, NC])
        x_bias = sb("x_bias", [P, NC])
        e_bias = sb("e_bias", [P, NC])
        e_part = sb("e_part", [P, NC, NPAIR])
        ex_part = sb("ex_part", [P, NC, NPAIR])
        e_sum = sb("e_sum", [P, NC])
        ex_sum = sb("ex_sum", [P, NC])
        g_vec = sb("g_vec", [P, NC])
        k_bias = sb("k_bias", [P, NO])
        v_bias = sb("v_bias", [P, TC])
        blk_max = sb("blk_max", [P, NJ])
        neg_max = sb("neg_max", [P, 2])
        row_sums = sb("row_sums", [P, 2, NCH])
        row_sum = sb("row_sum", [P, 1])
        row_inv = sb("row_inv", [P, 2])

        with ExitStack() as region:
            x_img = sb("x_img", [P, NC, HW], stack=region)
            e_img = sb("e_img", [P, 2, PAIR], stack=region)
            w_raw = sb("w_raw", [P, NW, TC], stack=region)
            wg_raw = sb("wg_raw", [P, 2 * NC, TC], stack=region)
            g_wide = sb("g_wide", [P, NC, P], stack=region)
            x_hi_odd = sb("x_hi_odd", [P, NC, BLK], F32R, region)
            x_lo_odd = sb("x_lo_odd", [P, NC, BLK], F32R, region)
        k_hi = sb("k_hi", [P, NO, HW], F32R)
        k_lo = sb("k_lo", [P, NO, HW], F32R)
        v_hl = sb("v_hl", [P, NT, 2 * TC], F32R)

        with ExitStack() as region:
            w_hi = sb("w_hi", [P, NW, TC], F32R, region)
            w_lo = sb("w_lo", [P, NW, TC], F32R, region)
            x_blk = sb("x_blk", [P, NC, BLK], F32, region)
            x_hi = sb("x_hi", [P, NC, BLK], F32R, region)
            x_lo = sb("x_lo", [P, NC, BLK], F32R, region)
            h_hi = sb("h_hi", [P, NO, BLK], F32R, region)
            h_lo = sb("h_lo", [P, NO, BLK], F32R, region)
            lin = sb("lin", [P, 2 * NO, BLK], F32, region)
            v_tmp = sb("v_tmp", [P, TC], F32, region)
        q_raw = sb("q_raw", [P, 2, NO, P])
        q_hi = sb("q_hi", [P, 2, NO, P], F32R)
        q_lo = sb("q_lo", [P, 2, NO, P], F32R)
        probs = sb("probs", [P, 2, CHUNK])
        ctx_part = sb("ctx_part", [P, TC])
        ctx_row = sb("ctx_row", [P, TC])
        x_res = sb("x_res", [P, 2, BLK])
        scores = sb("scores", [P, HW])
        pt_hi = sb("pt_hi", [P, RING_PT, BLK], F32R)
        pt_lo = sb("pt_lo", [P, RING_PT, BLK], F32R)
        ct_hi = sb("ct_hi", [P, NO, BLK], F32R)
        ct_lo = sb("ct_lo", [P, NO, BLK], F32R)
        wo_hi = sb("wo_hi", [P, NO, C], F32R)
        wo_lo = sb("wo_lo", [P, NO, C], F32R)
        y_out = sb("y_out", [P, RING_Y, BLK])

        q_dram = nc.dram_tensor("q_scratch", (BATCH, NO, P, HW), F32, kind="Internal").ap()

        ps = ctx.enter_context(nc.psum_tensor("ps", [P, 8, BLK], F32))
        S_BANK, T_BANK, CTX_BANK, CT_BANK, O_BANK, V_BANK = 0, 2, 4, 6, 7, 4

        const_in = sem("const_in")
        img_in = [sem("img_in0"), sem("img_in1")]
        img_ready = sem("img_ready")
        wq_in, wkv_in, wg_in, wo_in = sem("wq_in"), sem("wkv_in"), sem("wg_in"), sem("wo_in")
        wq_hi_done, wq_split, wkv_hi_done, wkv_split = (
            sem("wq_hi_done"), sem("wq_split"), sem("wkv_hi_done"), sem("wkv_split"))
        wo_hi_done, wo_split = sem("wo_hi_done"), sem("wo_split")
        first_stats = sem("first_stats")
        stat_step = sem("stat_step")
        piece_in, piece_read = sem("piece_in"), sem("piece_read")
        mean_ready, var_ready = sem("mean_ready"), sem("var_ready")
        stat_mean, stat_var, ve_ready, sqrt_done = (
            sem("stat_mean"), sem("stat_var"), sem("ve_ready"), sem("sqrt_done"))
        coef_ready, e_bias_ready, e_done, ex_done, g_ready, glob_ready, glob_done = (
            sem("coef_ready"), sem("e_bias_ready"), sem("e_done"), sem("ex_done"), sem("g_ready"),
            sem("glob_ready"), sem("glob_done"))
        x_in = [sem("x_in0"), sem("x_in1")]
        x_arrived = sem("x_arrived")
        xq_norm, xkv_norm, xh_ready, xl_ready = sem("xq_norm"), sem("xkv_norm"), sem("xh_ready"), sem("xl_ready")
        q1_ready, q2_ready, k1_ready, k2_ready = sem("q1_ready"), sem("q2_ready"), sem("k1_ready"), sem("k2_ready")
        q1_out, q2_out, k1_out, k2_out = sem("q1_out"), sem("q2_out"), sem("k1_out"), sem("k2_out")
        h_hi_done, h_split, k_hi_done, k_split = sem("h_hi_done"), sem("h_split"), sem("k_hi_done"), sem("k_split")
        v_ready, v_read, v_biased, v_hi_done, v_split = (
            sem("v_ready"), sem("v_read"), sem("v_biased"), sem("v_hi_done"), sem("v_split"))
        q_stored = sem("q_stored")
        q_in = [sem("q_in0"), sem("q_in1")]
        q_hi_done, q_split = sem("q_hi_done"), sem("q_split")
        scores_ready, scores_copied, max_ready, probs_ready = (
            sem("scores_ready"), sem("scores_copied"), sem("max_ready"), sem("probs_ready"))
        tposed, pt_hi_done, pt_split, pv_done = sem("tposed"), sem("pt_hi_done"), sem("pt_split"), sem("pv_done")
        sum_done, inv_ready, part_ready, ctx_ready = (
            sem("sum_done"), sem("inv_ready"), sem("part_ready"), sem("ctx_ready"))
        ct_ready, ct_hi_done, ct_split = sem("ct_ready"), sem("ct_hi_done"), sem("ct_split")
        o_ready, o_relu, y_ready = sem("o_ready"), sem("o_relu"), sem("y_ready")
        x_res_in = [sem("x_res_in0"), sem("x_res_in1")]
        y_stored = [sem(f"y_stored{s}") for s in range(RING_Y)]

        slot_stores = [len(range(s, NC, RING_Y)) for s in range(RING_Y)]

        block = ctx.enter_context(nc.Block())

        def key_cols(j):
            return slice(j * BLK, (j + 1) * BLK)

        def q_half(b, n, h):
            return b * (4 * NBLK) + n * 2 + h

        def kv_half(b, blk, h):
            return b * (4 * NBLK) + 2 * NBLK + blk * 2 + h

        def results(b, n, oc):
            return b * (NBLK * NO) + n * NO + oc

        @block.gpsimd
        def _(pool):
            for s in (xl_ready, q1_ready, q2_ready, q1_out, q2_out, h_split, k_split, v_read, v_split,
                      q_stored, scores_ready, scores_copied, max_ready, probs_ready, tposed, pt_split,
                      pv_done, inv_ready, part_ready, ctx_ready, ct_ready, ct_split, o_ready, o_relu, y_ready,
                      piece_read, e_done, ex_done, k1_out, k2_out,
                      *y_stored):
                pool.sem_inc(s, START)

            def add_residual(g, co):
                pool.wait_ge(o_relu, START + g * NC + co + 1)
                pool.wait_ge(x_res_in[co % 2], g * (16 * NC // 2) + 16 * (co // 2) + 16)
                nc.gpsimd.tensor_tensor(y_out[:, co % RING_Y], y_out[:, co % RING_Y], x_res[:, co % 2], ALU.add)\
                    .then_inc(y_ready, 1)

            def normalise(b, blk, h):
                pool.wait_ge(x_in[h], b * (16 * (NBLK - 1)) + blk * 16)
                pool.sem_inc(x_arrived, 1)
                cols = slice(h * HALF, (h + 1) * HALF)
                for c in range(NC):
                    last = nc.gpsimd.tensor_scalar(x_blk[:, c, cols], x_blk[:, c, cols], rstd[:, c:c + 1],
                                                   x_bias[:, c:c + 1], ALU.mult, ALU.add)
                last.then_inc(xkv_norm, 1)

            def h_low(b, n):
                for oc in range(NO):
                    pool.wait_ge(h_hi_done, 2 * results(b, 0, 0) + n * NO + oc + 1)
                    nc.gpsimd.tensor_tensor(h_lo[:, oc], lin[:, oc], h_hi[:, oc].bitcast(F32), ALU.subtract)\
                        .then_inc(h_split, 1)

            def kv_weights_low(b, pair):
                cols = bass.ds(pair * W_COLS, W_COLS)
                pool.wait_ge(wkv_hi_done, b * NPAIR + pair + 1)
                nc.gpsimd.tensor_tensor(w_lo[:, WK1:, cols], w_raw[:, WK1:, cols], w_hi[:, WK1:, cols].bitcast(F32),
                                        ALU.subtract).then_inc(wkv_split, 1)

            def image(b):
                h_low(b, 0)
                kv_weights_low(b, 0)
                with pool.Fori(1, NPAIR) as pair:
                    h_low(b, pair * 2 - 1)
                    h_low(b, pair * 2)
                    kv_weights_low(b, pair)
                h_low(b, NBLK - 1)
                with pool.Fori(1, NBLK) as blk:
                    for h in range(2):
                        normalise(b, blk, h)
                with pool.Fori(0, NBLK) as blk:
                    for co in range(NC):
                        add_residual(b * NBLK + blk, co)

            with pool.Fori(0, BATCH - 1) as b:
                image(b)
            image(BATCH - 1)

        @block.sync
        def _(sp):
            sp.dma_start(aff[:], affine).then_inc(const_in, 16)
            sp.dma_start(vaff[:], v_affine).then_inc(const_in, 16)
            sp.dma_start(ident[:], ident_in).then_inc(const_in, 16)
            sp.dma_start(group_mean[:], group_in).then_inc(const_in, 16)

            def load_pair(b, pair):
                sp.dma_start(x_img[:, :, pair * PAIR:(pair + 1) * PAIR],
                             x[bass.ds(b, 1), :, :, pair * PAIR:(pair + 1) * PAIR]
                             .rearrange("b c p n -> p (b c) n")).then_inc(img_in[pair % 2], 16)

            def load_weights(rows, done):
                sp.dma_start(w_raw[:, rows], w_proj.rearrange("(r p) o -> p r o", p=P)[:, rows]).then_inc(done, 16)

            def load_first(b):
                load_weights(slice(0, WK1), wq_in)
                load_pair(b, 0)
                load_pair(b, 1)
                load_weights(slice(WK1, NW), wkv_in)
                sp.dma_start(wg_raw[:], w_glob.rearrange("(r p) o -> p r o", p=P)).then_inc(wg_in, 16)

            def load_half(b, blk, h):
                sp.dma_start(x_blk[:, :, h * HALF:(h + 1) * HALF],
                             x[bass.ds(b, 1), :, :, bass.ds(blk * BLK + h * HALF, HALF)]
                             .rearrange("b c p n -> p (b c) n")).then_inc(x_in[h], 16)

            def store_q(b, n):
                for oc in range(NO):
                    sp.wait_ge(q2_out, START + results(b, n, oc) + 1)
                    sp.dma_start(q_dram[bass.ds(b, 1), oc, :, bass.ds(n * BLK, BLK)]
                                 .rearrange("b p n -> p (b n)"), lin[:, NO + oc, :]).then_inc(q_stored, 16)

            def load_q(b, tile, slot):
                sp.dma_start(q_raw[:, slot], q_dram[bass.ds(b, 1), :, :, bass.ds(tile * P, P)]
                             .rearrange("b o p n -> p (b o) n")).then_inc(q_in[slot], 16)

            def load_res(b, blk, co):
                sp.dma_start(x_res[:, co % 2], x[bass.ds(b, 1), co, :, bass.ds(blk * BLK, BLK)]
                             .rearrange("b p n -> p (b n)")).then_inc(x_res_in[co % 2], 16)

            def load_piece(b, blk, c):
                sp.dma_start(x_res[:, 0], x[1:][bass.ds(b, 1), c, :, bass.ds(blk * BLK, BLK)]
                             .rearrange("b p n -> p (b n)")).then_inc(piece_in, 16)

            def attend(b, blk, last, more_images):
                t0 = (b * NBLK + blk) * TPB
                y0 = (b * NBLK + blk) * NC
                sp.wait_ge(wo_split, b + 1)
                for i in range(TPB):
                    if more_images:
                        sp.wait_ge(piece_read, START + t0 + i)
                        load_piece(b, blk, i)
                    if not last or i < TPB - 2:
                        sp.wait_ge(q_split, t0 + i + 1)
                        load_q(b, blk * TPB + i + 2, i % 2)
                if more_images:
                    sp.wait_ge(piece_read, START + t0 + TPB)
                load_res(b, blk, 1)
                load_res(b, blk, 0)
                if last and more_images:
                    sp.wait_ge(pv_done, START + (b + 1) * (NT * NJ))
                    load_first(b + 1)
                for co in range(NC):
                    sp.wait_ge(y_ready, START + y0 + co + 1)
                    sp.dma_start(out[bass.ds(b, 1), co, :, bass.ds(blk * BLK, BLK)]
                                 .rearrange("b p n -> p (b n)"), y_out[:, co % RING_Y])\
                        .then_inc(y_stored[co % RING_Y], 16)
                    if co + 2 < NC:
                        load_res(b, blk, co + 2)

            def image(b, more_images):
                for pair in range(NPAIR):
                    sp.wait_ge(img_in[pair % 2], b * (16 * NPAIR // 2) + 16 * (pair // 2) + 16)
                    sp.sem_inc(img_ready, 1)
                    if pair + 2 < NPAIR:
                        load_pair(b, pair + 2)
                with sp.Fori(0, NPAIR) as pair:
                    for odd in range(2):
                        store_q(b, pair * 2 + odd)
                with sp.Fori(0, NBLK - 1) as blk:
                    for h in range(2):
                        sp.wait_ge(xl_ready, START + kv_half(b, blk, h) + 1)
                        load_half(b, blk + 1, h)
                sp.wait_ge(q_stored, START + (b + 1) * (16 * NO * NBLK))
                sp.dma_start(x_res[:], w_out.rearrange("(r p) o -> p r o", p=P)).then_inc(wo_in, 16)
                load_q(b, 0, 0)
                load_q(b, 1, 1)
                with sp.Fori(0, NBLK - 1) as blk:
                    attend(b, blk, False, more_images)
                attend(b, NBLK - 1, True, more_images)

            load_first(0)
            with sp.Fori(0, BATCH - 1) as b:
                image(b, True)
            image(BATCH - 1, False)
            for s in range(RING_Y):
                sp.wait_ge(y_stored[s], START + BATCH * 16 * NBLK * slot_stores[s])
            sp.wait_ge(q_stored, START + BATCH * 16 * NO * NBLK)

        @block.scalar
        def _(act):
            def x_high_block(b, n, hi):
                act.wait_ge(xq_norm, b * Q_STEPS + n + 1)
                act.wait_ge(q1_ready, START + results(b, n, 0) - 2 * NO)
                nc.scalar.copy(hi[:], x_blk[:]).then_inc(xh_ready, 2)

            def x_high_half(b, blk, h):
                act.wait_ge(xkv_norm, b * (2 * (NBLK - 1)) + 2 * (blk - 1) + h + 1)
                act.wait_ge(v_ready, (b * NBLK + blk) * TPB - TPB + 2 * (h + 1))
                cols = slice(h * HALF, (h + 1) * HALF)
                nc.scalar.copy(x_hi[:, :, cols], x_blk[:, :, cols]).then_inc(xh_ready, 1)

            def relu(bank, ready, out_sem, count, gain, bias):
                act.wait_ge(ready, count)
                nc.scalar.activation(lin[:, bank], ps[:, bank], ACT.Relu, bias=bias, scale=gain).then_inc(out_sem, 1)

            def finish_q1(b, n):
                act.wait_ge(h_split, START + 2 * results(b, 0, 0) + n * NO)
                for oc in range(NO):
                    relu(oc, q1_ready, q1_out, START + results(b, n, oc) + 1, aff[:, QG1 + oc:QG1 + oc + 1],
                         aff[:, QB1 + oc:QB1 + oc + 1])

            def finish_q2(b, n):
                act.wait_ge(q_stored, START + 16 * results(b, n, 0))
                for oc in range(NO):
                    relu(NO + oc, q2_ready, q2_out, START + results(b, n, oc) + 1, aff[:, QG2 + oc:QG2 + oc + 1],
                         aff[:, QB2 + oc:QB2 + oc + 1])

            def finish_k1(b, n):
                for oc in range(NO):
                    relu(oc, k1_ready, k1_out, results(b, n, oc) + 1, aff[:, KG1 + oc:KG1 + oc + 1],
                         k_bias[:, oc:oc + 1])

            def finish_k2(b, n):
                act.wait_ge(q_stored, START + b * (16 * NO * NBLK) + 16 * NO * NBLK)
                act.wait_ge(k_split, START + results(b, n, 0))
                for oc in range(NO):
                    relu(NO + oc, k2_ready, k2_out, results(b, n, oc) + 1, aff[:, KG2 + oc:KG2 + oc + 1],
                         aff[:, KB2 + oc:KB2 + oc + 1])

            def global_exp(b, pair, chunks):
                for c in chunks:
                    act.wait_ge(ex_done, START + (b * NPAIR + pair) * NC + c - 1)
                    nc.scalar.activation(e_img[:, c % 2], x_img[:, c, bass.ds(pair * PAIR, PAIR)], ACT.Exp,
                                         bias=e_bias[:, c:c + 1], scale=rstd[:, c:c + 1],
                                         accum_out=e_part[:, c, bass.ds(pair, 1)]).then_inc(e_done, 1)

            def kv_weights_high(pair):
                cols = bass.ds(pair * W_COLS, W_COLS)
                nc.scalar.copy(w_hi[:, WK1:, cols], w_raw[:, WK1:, cols]).then_inc(wkv_hi_done, 1)

            def kv_block(b, blk, last):
                finish_k1(b, blk)
                if last:
                    q_high(0, b * (NT // 2), b * (NJ * NT))
                    q_high(1, b * (NT // 2), b * (NJ * NT))
                else:
                    for h in range(2):
                        x_high_half(b, blk + 1, h)
                finish_k2(b, blk)

            def q_high(slot, pair, scored):
                act.wait_ge(q_in[slot], pair * 16 + 16)
                act.wait_ge(scores_ready, START + scored)
                nc.scalar.copy(q_hi[:, slot], q_raw[:, slot]).then_inc(q_hi_done, 1)

            def exponential(t, parity, c):
                if c == 0:
                    act.wait_ge(max_ready, START + t + 1)
                    act.wait_ge(inv_ready, START + t - 1)
                act.wait_ge(tposed, START + t * (2 * NCH) + 2 * c - 2)
                nc.scalar.activation(probs[:, c % 2], scores[:, c * CHUNK:(c + 1) * CHUNK], ACT.Exp,
                                     bias=neg_max[:, parity:parity + 1],
                                     accum_out=row_sums[:, parity, c:c + 1]).then_inc(probs_ready, 1)

            def pt_high(t, j):
                act.wait_ge(tposed, START + t * NJ + j + 1)
                act.wait_ge(pv_done, START + t * NJ + j + 1 - (2 if j < 2 else RING_PT))
                nc.scalar.copy(pt_hi[:, j % RING_PT], ps[:, T_BANK + j % RING_T]).then_inc(pt_hi_done, 1)

            def ctx_part_out(t, parity):
                act.wait_ge(pv_done, START + t * NJ + NJ)
                act.wait_ge(inv_ready, START + t + 1)
                act.wait_ge(ctx_ready, START + t)
                nc.scalar.activation(ctx_part[:], ps[:, CTX_BANK + parity, TC:2 * TC], ACT.Copy,
                                     scale=row_inv[:, parity:parity + 1]).then_inc(part_ready, 1)

            def ct_high(t, y0, i):
                act.wait_ge(ct_ready, START + t + 1)
                if i == 0:
                    act.wait_ge(o_ready, START + y0)
                nc.scalar.copy(ct_hi[:, :, i * P:(i + 1) * P], ps[:, CT_BANK, 0:TC].rearrange("p (o n) -> p o n", o=NO))\
                    .then_inc(ct_hi_done, 1)

            def project_out(g, co):
                act.wait_ge(o_ready, START + g * NC + co + 1)
                act.wait_ge(y_stored[co % RING_Y], START + g * (16 * slot_stores[co % RING_Y])
                            + 16 * (co // RING_Y))
                nc.scalar.activation(y_out[:, co % RING_Y], ps[:, O_BANK - co % 2], ACT.Relu,
                                     bias=aff[:, OB + co:OB + co + 1], scale=aff[:, OG + co:OG + co + 1])\
                    .then_inc(o_relu, 1)

            def attend(b, blk, last):
                g = b * NBLK + blk
                for i in range(TPB):
                    t = g * TPB + i
                    more = not last or i < TPB - 1
                    for j in range(NJ):
                        pt_high(t, j)
                        if j in (1, 3):
                            exponential(t, i % 2, 2 + j // 2)
                        if i > 0 and j == 2:
                            ctx_part_out(t - 1, (i - 1) % 2)
                        if i > 0 and j == 4:
                            ct_high(t - 1, g * NC, i - 1)
                        if j == 5 and (not last or i < TPB - 2):
                            q_high(i % 2, g * (TPB // 2) + i // 2 + 1, t * NJ + NJ)
                    if i == TPB - 1:
                        ctx_part_out(t, i % 2)
                        ct_high(t, g * NC, i)
                    if i == TPB - 1:
                        project_out(g, 0)
                        project_out(g, 1)
                    if more:
                        exponential(t + 1, (i + 1) % 2, 0)
                        exponential(t + 1, (i + 1) % 2, 1)
                for co in range(2, NC):
                    project_out(g, co)

            def image(b):
                act.wait_ge(wq_in, b * 16 + 16)
                nc.scalar.copy(w_hi[:, 0:WK1], w_raw[:, 0:WK1]).then_inc(wq_hi_done, 1)
                act.wait_ge(ve_ready, b + 1)
                nc.scalar.activation(small[:, 1], small[:, 0], ACT.Sqrt).then_inc(sqrt_done, 1)
                x_high_block(b, 0, x_hi)
                act.wait_ge(e_bias_ready, b + 1)
                global_exp(b, 0, (0, 1))
                x_high_block(b, 1, x_hi_odd)
                for s in range(RING_Y):
                    act.wait_ge(y_stored[s], START + b * (16 * NBLK * slot_stores[s]))
                finish_q1(b, 0)
                global_exp(b, 0, (2, 3))
                act.wait_ge(wkv_in, b * 16 + 16)
                kv_weights_high(0)
                with act.Fori(1, NPAIR) as pair:
                    n = pair * 2
                    x_high_block(b, n, x_hi)
                    act.wait_ge(img_ready, b * NPAIR + pair + 1)
                    global_exp(b, pair, (0, 1))
                    finish_q1(b, n - 1)
                    finish_q2(b, n - 2)
                    x_high_block(b, n + 1, x_hi_odd)
                    global_exp(b, pair, (2, 3))
                    finish_q1(b, n)
                    finish_q2(b, n - 1)
                    kv_weights_high(pair)
                x_high_block(b, NBLK, x_hi)
                finish_q1(b, NBLK - 1)
                finish_q2(b, NBLK - 2)
                finish_q2(b, NBLK - 1)
                act.wait_ge(glob_done, b + 1)
                with act.Fori(0, NBLK - 1) as blk:
                    kv_block(b, blk, False)
                kv_block(b, NBLK - 1, True)
                exponential(b * NT, 0, 0)
                exponential(b * NT, 0, 1)
                act.wait_ge(wo_in, b * 16 + 16)
                nc.scalar.copy(wo_hi[:], x_res[:]).then_inc(wo_hi_done, 1)
                with act.Fori(0, NBLK - 1) as blk:
                    attend(b, blk, False)
                attend(b, NBLK - 1, True)

            act.wait_ge(const_in, 64)
            with act.Fori(0, BATCH - 1) as b:
                image(b)
            image(BATCH - 1)

        @block.tensor
        def _(pe):
            def three(out_ap, terms, done):
                n = len(terms)
                for k, (w, m) in enumerate(terms):
                    last = nc.tensor.matmul(out_ap, w, m, start=(k == 0), stop=(k == n - 1))
                last.then_inc(done, 1)

            def linear(bank, row, chunks, oc, hi, lo, done):
                cols = slice(oc * P, (oc + 1) * P)
                terms = []
                for c in range(chunks):
                    terms += [(w_hi[:, row + c, cols], hi[:, c]), (w_lo[:, row + c, cols], hi[:, c]),
                              (w_hi[:, row + c, cols], lo[:, c])]
                three(ps[:, bank], terms, done)

            def q1(b, n, hi, lo):
                pe.wait_ge(xl_ready, START + q_half(b, n, 1) + 1)
                for oc in range(NO):
                    pe.wait_ge(q1_out, START + results(b, n, oc) + 1 - NO)
                    linear(oc, WQ1, NC, oc, hi, lo, q1_ready)

            def q2(b, n):
                pe.wait_ge(h_split, START + 2 * results(b, 0, 0) + n * NO + NO)
                for oc in range(NO):
                    pe.wait_ge(q2_out, START + results(b, n, oc) + 1 - NO)
                    linear(NO + oc, WQ2, NO, oc, h_hi, h_lo, q2_ready)

            def kv_block(b, blk):
                pe.wait_ge(xl_ready, START + kv_half(b, blk, 1) + 1)
                for oc in range(NO):
                    pe.wait_ge(k1_out, START + results(b, blk, oc) + 1 - NO)
                    linear(oc, WK1, NC, oc, x_hi, x_lo, k1_ready)
                for u in range(TPB):
                    values(b * NBLK + blk, u)
                pe.wait_ge(h_split, START + 2 * results(b, 0, 0) + NBLK * NO + blk * NO + NO)
                for oc in range(NO):
                    pe.wait_ge(k2_out, START + results(b, blk, oc) + 1 - NO)
                    linear(NO + oc, WK2, NO, oc, h_hi, h_lo, k2_ready)

            def values(g, u):
                pe.wait_ge(v_read, START + g * TPB + u + 1 - RING_V)
                cols = slice(u * P, (u + 1) * P)
                terms = []
                for c in range(NC):
                    terms += [(x_hi[:, c, cols], w_hi[:, WV + c]), (x_hi[:, c, cols], w_lo[:, WV + c]),
                              (x_lo[:, c, cols], w_hi[:, WV + c])]
                three(ps[:, V_BANK + u % RING_V, 0:TC], terms, v_ready)

            def score(t, slot, j):
                pe.wait_ge(scores_copied, START + t * NJ + j + 1 - RING_S)
                terms = []
                for c in range(NO):
                    terms += [(q_hi[:, slot, c], k_hi[:, c, key_cols(j)]), (q_hi[:, slot, c], k_lo[:, c, key_cols(j)]),
                              (q_lo[:, slot, c], k_hi[:, c, key_cols(j)])]
                three(ps[:, S_BANK + j % RING_S], terms, scores_ready)

            def turn(t, j):
                if j % 2 == 0:
                    pe.wait_ge(probs_ready, START + t * NCH + j // 2 + 1)
                pe.wait_ge(pt_split, START + t * NJ + j + 1 - RING_T)
                for k in range(BLK // P):
                    at = (j % 2) * BLK + k * P
                    last = nc.tensor.transpose(ps[:, T_BANK + j % RING_T, k * P:(k + 1) * P],
                                               probs[:, (j // 2) % 2, at:at + P], ident[:])
                last.then_inc(tposed, 1)

            def context(t, parity, j):
                if j == 0:
                    pe.wait_ge(ctx_ready, START + t + 1 - RING_CTX)
                pe.wait_ge(pt_split, START + t * NJ + j + 1)
                bank = ps[:, CTX_BANK + parity]
                for k in range(BLK // P):
                    m = j * (BLK // P) + k
                    cols = slice(k * P, (k + 1) * P)
                    nc.tensor.matmul(bank, pt_hi[:, j % RING_PT, cols], v_hl[:, m], start=(m == 0), stop=False)
                    last = nc.tensor.matmul(bank[:, 0:TC], pt_lo[:, j % RING_PT, cols], v_hl[:, m, 0:TC],
                                            start=False, stop=(m == NT - 1))
                last.then_inc(pv_done, 1)

            def turn_context(t, y0, i):
                pe.wait_ge(ctx_ready, START + t + 1)
                pe.wait_ge(ct_split, START + t)
                if i == 0:
                    pe.wait_ge(o_relu, START + y0)
                for c in range(NO):
                    last = nc.tensor.transpose(ps[:, CT_BANK, c * P:(c + 1) * P], ctx_row[:, c * P:(c + 1) * P], ident[:])
                last.then_inc(ct_ready, 1)

            def project_out(g, co):
                if co == 0:
                    pe.wait_ge(ct_split, START + g * TPB + TPB)
                pe.wait_ge(o_relu, START + g * NC + (co - 1 if co >= 2 else 0))
                cols = slice(co * P, (co + 1) * P)
                terms = []
                for c in range(NO):
                    terms += [(wo_hi[:, c, cols], ct_hi[:, c]), (wo_lo[:, c, cols], ct_hi[:, c]),
                              (wo_hi[:, c, cols], ct_lo[:, c])]
                three(ps[:, O_BANK - co % 2], terms, o_ready)

            def attend(b, blk, last):
                g = b * NBLK + blk
                for i in range(TPB):
                    t = g * TPB + i
                    more = not last or i < TPB - 1
                    own = i == TPB - 1
                    if more:
                        pe.wait_ge(q_split, t + 2)
                    for j in range(NJ - 1):
                        if more and not (own and j >= HELD):
                            score(t + 1, (i + 1) % 2, j)
                        turn(t, j)
                        if own and j == NJ - 2:
                            turn(t, NJ - 1)
                        if j > 0:
                            context(t, i % 2, j - 1)
                        if i > 0 and j == 3:
                            turn_context(t - 1, g * NC, i - 1)
                    if not own:
                        turn(t, NJ - 1)
                        if more:
                            score(t + 1, (i + 1) % 2, NJ - 1)
                    context(t, i % 2, NJ - 2)
                    context(t, i % 2, NJ - 1)
                    if own:
                        if more:
                            score(t + 1, (i + 1) % 2, HELD)
                        turn_context(t, g * NC, i)
                        if more:
                            for j in range(HELD + 1, NJ):
                                score(t + 1, (i + 1) % 2, j)
                        for co in range(NC):
                            project_out(g, co)

            def image(b):
                pe.wait_ge(stat_mean, b + 1)
                pe.wait_ge(o_relu, START + b * (NBLK * NC))
                nc.tensor.matmul(ps[:, 7, 0:NC], group_mean[:], small[:, 2], start=True, stop=True)\
                    .then_inc(mean_ready, 1)
                pe.wait_ge(stat_var, b + 1)
                nc.tensor.matmul(ps[:, 7, 0:NC], group_mean[:], small[:, 3], start=True, stop=True)\
                    .then_inc(var_ready, 1)
                pe.wait_ge(wq_split, b + 1)
                q1(b, 0, x_hi, x_lo)
                q1(b, 1, x_hi_odd, x_lo_odd)
                q2(b, 0)
                with pe.Fori(1, NPAIR) as pair:
                    n = pair * 2
                    q1(b, n, x_hi, x_lo)
                    q2(b, n - 1)
                    q1(b, n + 1, x_hi_odd, x_lo_odd)
                    q2(b, n)
                q2(b, NBLK - 1)
                pe.wait_ge(g_ready, b + 1)
                pe.wait_ge(wg_in, b * 16 + 16)
                for oc in range(NO):
                    for c in range(NC):
                        nc.tensor.matmul(ps[:, 7, 8 + oc:9 + oc], wg_raw[:, c, oc * P:(oc + 1) * P], g_vec[:, c:c + 1],
                                         start=(c == 0), stop=(c == NC - 1))
                for c in range(NC):
                    last = nc.tensor.matmul(ps[:, 6, 0:TC], g_wide[:, c], wg_raw[:, NC + c], start=(c == 0),
                                            stop=(c == NC - 1))
                last.then_inc(glob_ready, 1)
                pe.wait_ge(wkv_split, (b + 1) * NPAIR)
                with pe.Fori(0, NBLK) as blk:
                    kv_block(b, blk)
                pe.wait_ge(q_split, b * NT + 1)
                for j in range(NJ):
                    if j == 0 or j == NJ - 1:
                        pe.wait_ge(k_split, START + results(b, NBLK - 1 + (j == NJ - 1), 0))
                    score(b * NT, 0, j)
                with pe.Fori(0, NBLK - 1) as blk:
                    attend(b, blk, False)
                attend(b, NBLK - 1, True)

            pe.wait_ge(const_in, 64)
            with pe.Fori(0, BATCH - 1) as b:
                image(b)
            image(BATCH - 1)

        @block.vector
        def _(dve):
            def x_normalise(b, n, source):
                dve.wait_ge(xl_ready, START + q_half(b, n, 0))
                for c in range(NC):
                    last = nc.vector.tensor_scalar(x_blk[:, c], source(c), rstd[:, c:c + 1], x_bias[:, c:c + 1],
                                                   ALU.mult, ALU.add)
                last.then_inc(xq_norm, 1)

            def x_low_block(b, n, hi, lo):
                dve.wait_ge(xh_ready, q_half(b, n, 1) + 1)
                nc.vector.tensor_tensor(lo[:], x_blk[:], hi[:].bitcast(F32), ALU.subtract).then_inc(xl_ready, 2)

            def x_low_half(b, blk, h):
                dve.wait_ge(xh_ready, kv_half(b, blk, h) + 1)
                cols = slice(h * HALF, (h + 1) * HALF)
                nc.vector.tensor_tensor(x_lo[:, :, cols], x_blk[:, :, cols], x_hi[:, :, cols].bitcast(F32),
                                        ALU.subtract).then_inc(xl_ready, 1)

            def q1_high(b, n):
                dve.wait_ge(q2_ready, START + results(b, n, 0))
                for oc in range(NO):
                    dve.wait_ge(q1_out, START + results(b, n, oc) + 1)
                    nc.vector.tensor_copy(h_hi[:, oc], lin[:, oc]).then_inc(h_hi_done, 1)

            def split_k1(b, blk):
                for oc in range(NO):
                    dve.wait_ge(k1_out, START + results(b, blk, oc) + 1)
                    nc.vector.tensor_copy(h_hi[:, oc], lin[:, oc]).then_inc(h_hi_done, 1)
                    dve.wait_ge(h_hi_done, 2 * results(b, 0, 0) + NBLK * NO + blk * NO + oc + 1)
                    nc.vector.tensor_tensor(h_lo[:, oc], lin[:, oc], h_hi[:, oc].bitcast(F32), ALU.subtract)\
                        .then_inc(h_split, 1)

            def split_k(b, blk, oc):
                cols = bass.ds(blk * BLK, BLK)
                dve.wait_ge(k2_out, START + results(b, blk, oc) + 1)
                nc.vector.tensor_copy(k_hi[:, oc, cols], lin[:, NO + oc]).then_inc(k_hi_done, 1)
                dve.wait_ge(k_hi_done, results(b, blk, oc) + 1)
                nc.vector.tensor_tensor(k_lo[:, oc, cols], lin[:, NO + oc], k_hi[:, oc, cols].bitcast(F32),
                                        ALU.subtract).then_inc(k_split, 1)

            def split_v(g, blk, u):
                n = g * TPB + u
                dve.wait_ge(v_ready, n + 1)
                dve.wait_ge(v_split, START + n)
                nc.vector.tensor_tensor(v_tmp[:], ps[:, V_BANK + u % RING_V, 0:TC], vaff[:, 0], ALU.mult)\
                    .then_inc(v_read, 1)
                dve.wait_ge(v_read, START + n + 1)
                nc.vector.tensor_tensor(v_tmp[:], v_tmp[:], v_bias[:], ALU.add).then_inc(v_biased, 1)
                dve.wait_ge(v_biased, n + 1)
                m = blk * TPB + u
                hi = v_hl[:, bass.ds(m, 1), 0:TC].rearrange("p a c -> p (a c)")
                lo = v_hl[:, bass.ds(m, 1), TC:2 * TC].rearrange("p a c -> p (a c)")
                nc.vector.tensor_scalar(hi, v_tmp[:], 0.0, None, ALU.max).then_inc(v_hi_done, 1)
                dve.wait_ge(v_hi_done, n + 1)
                nc.vector.scalar_tensor_tensor(out=lo, in0=v_tmp[:], scalar=0.0, in1=hi.bitcast(F32), op0=ALU.max,
                                               op1=ALU.subtract).then_inc(v_split, 1)

            def kv_block(b, blk, last):
                g = b * NBLK + blk
                split_k1(b, blk)
                if last:
                    q_low(b * NT, 0)
                    q_low(b * NT + 1, 1)
                split_v(g, blk, 0)
                split_v(g, blk, 1)
                if not last:
                    x_low_half(b, blk + 1, 0)
                split_v(g, blk, 2)
                if not last:
                    x_low_half(b, blk + 1, 1)
                split_v(g, blk, 3)
                split_k(b, blk, 0)
                split_k(b, blk, 1)

            def global_sum(b, pair, chunks):
                for c in chunks:
                    dve.wait_ge(e_done, START + (b * NPAIR + pair) * NC + c + 1)
                    nc.vector.scalar_tensor_tensor(out=e_img[:, c % 2], in0=e_img[:, c % 2], scalar=1.0,
                                                   in1=x_img[:, c, bass.ds(pair * PAIR, PAIR)], op0=ALU.mult,
                                                   op1=ALU.mult, accum_out=ex_part[:, c, bass.ds(pair, 1)])\
                        .then_inc(ex_done, 1)

            def piece_stats(b, blk, c):
                dve.wait_ge(piece_in, (b * NBLK + blk) * (16 * TPB) + 16 * c + 16)
                nc.vector.tensor_reduce(max_part[:, c, bass.ds(blk, 1)], x_res[:, 0], AX.X, ALU.max)
                nc.vector.bn_stats(bn_part[:, c, bass.ds(blk, 1)].rearrange("p a s -> p (a s)"), x_res[:, 0])\
                    .then_inc(piece_read, 1)

            def copy_scores(t, j):
                if j % 2 == 0:
                    dve.wait_ge(probs_ready, START + (t - 1) * NCH + j // 2 + 1)
                if j == 0:
                    dve.wait_ge(max_ready, START + t)
                dve.wait_ge(scores_ready, START + t * NJ + j + 1)
                nc.vector.tensor_scalar(scores[:, key_cols(j)], ps[:, S_BANK + j % RING_S], SCALE, None, ALU.mult,
                                        ALU.max, accum_out=blk_max[:, j:j + 1]).then_inc(scores_copied, 1)

            def row_max(t, parity):
                dve.wait_ge(scores_copied, START + t * NJ + NJ)
                nc.vector.tensor_reduce(neg_max[:, parity:parity + 1], blk_max[:], AX.X, ALU.max, negate=True)\
                    .then_inc(max_ready, 1)

            def pt_low(t, j):
                dve.wait_ge(pt_hi_done, t * NJ + j + 1)
                nc.vector.tensor_tensor(pt_lo[:, j % RING_PT], ps[:, T_BANK + j % RING_T],
                                        pt_hi[:, j % RING_PT].bitcast(F32), ALU.subtract).then_inc(pt_split, 1)

            def row_inverse(t, parity):
                dve.wait_ge(probs_ready, START + t * NCH + NCH)
                dve.wait_ge(inv_ready, START + t)
                nc.vector.tensor_reduce(row_sum[:], row_sums[:, parity], AX.X, ALU.add).then_inc(sum_done, 1)
                dve.wait_ge(sum_done, t + 1)
                dve.wait_ge(part_ready, START + t - 1)
                nc.vector.reciprocal(row_inv[:, parity:parity + 1], row_sum[:]).then_inc(inv_ready, 1)

            def finish_context(t, parity):
                dve.wait_ge(part_ready, START + t + 1)
                dve.wait_ge(ct_ready, START + t)
                nc.vector.scalar_tensor_tensor(out=ctx_row[:], in0=ps[:, CTX_BANK + parity, 0:TC],
                                               scalar=row_inv[:, parity:parity + 1], in1=ctx_part[:],
                                               op0=ALU.mult, op1=ALU.add).then_inc(ctx_ready, 1)

            def ct_low(t, i):
                dve.wait_ge(ct_hi_done, t + 1)
                nc.vector.tensor_tensor(ct_lo[:, :, i * P:(i + 1) * P],
                                        ps[:, CT_BANK, 0:TC].rearrange("p (o n) -> p o n", o=NO),
                                        ct_hi[:, :, i * P:(i + 1) * P].bitcast(F32), ALU.subtract).then_inc(ct_split, 1)

            def q_low(t, slot):
                dve.wait_ge(q_hi_done, t + 1)
                nc.vector.tensor_tensor(q_lo[:, slot], q_raw[:, slot], q_hi[:, slot].bitcast(F32), ALU.subtract)\
                    .then_inc(q_split, 1)

            def attend(b, blk, last, more_images):
                g = b * NBLK + blk
                for i in range(TPB):
                    t = g * TPB + i
                    more = not last or i < TPB - 1
                    own = i == TPB - 1
                    for j in range(NJ):
                        if more_images and j == 3:
                            piece_stats(b, blk, i)
                        if more and j < (HELD if own else NJ - 1):
                            copy_scores(t + 1, j)
                        pt_low(t, j)
                        if more and not own and j == NJ - 1:
                            copy_scores(t + 1, j)
                            row_max(t + 1, (i + 1) % 2)
                        if i > 0 and j == 2:
                            finish_context(t - 1, (i - 1) % 2)
                        if i > 0 and j == 4:
                            ct_low(t - 1, i - 1)
                        if j == 4:
                            row_inverse(t, i % 2)
                        if j == 5 and (not last or i < TPB - 2):
                            q_low(t + 2, i % 2)
                    if own:
                        finish_context(t, i % 2)
                        if more:
                            copy_scores(t + 1, HELD)
                        ct_low(t, i)
                        if more:
                            for j in range(HELD + 1, NJ):
                                copy_scores(t + 1, j)
                            row_max(t + 1, (i + 1) % 2)

            STEPS = 18
            done = [0]

            def link(b, ins):
                done[0] += 1
                ins.then_inc(stat_step, 1)
                dve.wait_ge(stat_step, b * STEPS + done[0])

            def image(b, more_images):
                done[0] = 0
                nc.vector.tensor_reduce(x_max[:], max_part[:], AX.X, ALU.max)
                for c in range(NC):
                    last = nc.vector.bn_aggr(mean_var[:, c], bn_part[:, c])
                link(b, last)
                nc.vector.tensor_copy(small[:, 2], mean_var[:, :, 0]).then_inc(stat_mean, 1)
                dve.wait_ge(mean_ready, b + 1)
                link(b, nc.vector.tensor_copy(mean_g[:], ps[:, 7, 0:NC]))
                link(b, nc.vector.tensor_tensor(small[:, 4], mean_var[:, :, 0], mean_g[:], ALU.subtract))
                link(b, nc.vector.tensor_tensor(small[:, 4], small[:, 4], small[:, 4], ALU.mult))
                nc.vector.tensor_tensor(small[:, 3], small[:, 4], mean_var[:, :, 1], ALU.add).then_inc(stat_var, 1)
                dve.wait_ge(var_ready, b + 1)
                nc.vector.tensor_scalar(small[:, 0], ps[:, 7, 0:NC], EPS, None, ALU.add).then_inc(ve_ready, 1)
                dve.wait_ge(sqrt_done, b + 1)
                link(b, nc.vector.reciprocal(small[:, 4], small[:, 1]))
                link(b, nc.vector.tensor_tensor(small[:, 5], small[:, 4], small[:, 4], ALU.mult))
                link(b, nc.vector.tensor_tensor(small[:, 5], small[:, 5], small[:, 0], ALU.mult))
                link(b, nc.vector.tensor_scalar(small[:, 5], small[:, 5], -0.5, 1.5, ALU.mult, ALU.add))
                link(b, nc.vector.tensor_tensor(rstd[:], small[:, 4], small[:, 5], ALU.mult))
                nc.vector.scalar_tensor_tensor(out=x_bias[:], in0=mean_g[:], scalar=-1.0, in1=rstd[:], op0=ALU.mult,
                                               op1=ALU.mult).then_inc(coef_ready, 1)
                nc.vector.scalar_tensor_tensor(out=e_bias[:], in0=x_max[:], scalar=-1.0, in1=rstd[:], op0=ALU.mult,
                                               op1=ALU.mult).then_inc(e_bias_ready, 1)
                dve.wait_ge(wq_hi_done, b + 1)
                dve.wait_ge(y_ready, START + b * (NBLK * NC))
                nc.vector.tensor_tensor(w_lo[:, 0:WK1], w_raw[:, 0:WK1], w_hi[:, 0:WK1].bitcast(F32), ALU.subtract)\
                    .then_inc(wq_split, 1)
                def image_block(n):
                    return lambda c: x_img[:, c, bass.ds(n * BLK, BLK)]

                dve.wait_ge(coef_ready, b + 1)
                dve.wait_ge(img_ready, b * NPAIR + 1)
                x_normalise(b, 0, image_block(0))
                x_low_block(b, 0, x_hi, x_lo)
                x_normalise(b, 1, image_block(1))
                x_low_block(b, 1, x_hi_odd, x_lo_odd)
                global_sum(b, 0, (0, 1))
                q1_high(b, 0)
                with dve.Fori(1, NPAIR) as pair:
                    n = pair * 2
                    dve.wait_ge(img_ready, b * NPAIR + pair + 1)
                    x_normalise(b, n, image_block(n))
                    global_sum(b, pair - 1, (2, 3))
                    x_low_block(b, n, x_hi, x_lo)
                    q1_high(b, n - 1)
                    x_normalise(b, n + 1, image_block(n + 1))
                    global_sum(b, pair, (0, 1))
                    x_low_block(b, n + 1, x_hi_odd, x_lo_odd)
                    q1_high(b, n)
                x_normalise(b, NBLK, image_block(0))
                global_sum(b, NPAIR - 1, (2, 3))
                x_low_block(b, NBLK, x_hi, x_lo)
                q1_high(b, NBLK - 1)
                dve.wait_ge(ex_done, START + (b + 1) * (NPAIR * NC))
                nc.vector.tensor_reduce(e_sum[:], e_part[:], AX.X, ALU.add)
                link(b, nc.vector.tensor_reduce(ex_sum[:], ex_part[:], AX.X, ALU.add))
                link(b, nc.vector.reciprocal(small[:, 4], e_sum[:]))
                link(b, nc.vector.tensor_tensor(small[:, 4], small[:, 4], ex_sum[:], ALU.mult))
                link(b, nc.vector.tensor_tensor(small[:, 4], small[:, 4], mean_g[:], ALU.subtract))
                link(b, nc.vector.scalar_tensor_tensor(out=g_vec[:], in0=small[:, 4], scalar=1.0 / HW, in1=rstd[:],
                                                       op0=ALU.mult, op1=ALU.mult))
                for c in range(NC):
                    last = nc.vector.tensor_scalar(g_wide[:, c], group_mean[:], 0.0, g_vec[:, c:c + 1], ALU.mult,
                                                   ALU.add)
                last.then_inc(g_ready, 1)
                dve.wait_ge(glob_ready, b + 1)
                nc.vector.tensor_tensor(k_bias[:], ps[:, 7, 8:8 + NO], aff[:, KG1:KG1 + NO], ALU.mult)
                link(b, nc.vector.tensor_tensor(v_bias[:], ps[:, 6, 0:TC], vaff[:, 0], ALU.mult))
                nc.vector.tensor_tensor(k_bias[:], k_bias[:], aff[:, KB1:KB1 + NO], ALU.add)
                nc.vector.tensor_tensor(v_bias[:], v_bias[:], vaff[:, 1], ALU.add).then_inc(glob_done, 1)
                assert done[0] <= STEPS, done[0]
                for _ in range(STEPS - done[0]):
                    dve.sem_inc(stat_step, 1)
                dve.wait_ge(glob_done, b + 1)
                with dve.Fori(0, NBLK - 1) as blk:
                    kv_block(b, blk, False)
                kv_block(b, NBLK - 1, True)
                for j in range(NJ):
                    copy_scores(b * NT, j)
                row_max(b * NT, 0)
                dve.wait_ge(wo_hi_done, b + 1)
                nc.vector.tensor_tensor(wo_lo[:], x_res[:], wo_hi[:].bitcast(F32), ALU.subtract).then_inc(wo_split, 1)
                with dve.Fori(0, NBLK - 1) as blk:
                    attend(b, blk, False, more_images)
                attend(b, NBLK - 1, True, more_images)

            dve.wait_ge(const_in, 64)
            for pair in range(NPAIR):
                dve.wait_ge(img_ready, pair + 1)
                for c in range(NC):
                    for n in (2 * pair, 2 * pair + 1):
                        nc.vector.bn_stats(bn_part[:, c, n], x_img[:, c, key_cols(n)])
                for n in (2 * pair, 2 * pair + 1):
                    last = nc.vector.tensor_reduce(max_part[:, :, n], x_img[:, :, key_cols(n)], AX.X, ALU.max)
            last.then_inc(first_stats, 1)
            dve.wait_ge(first_stats, 1)
            with dve.Fori(0, BATCH - 1) as b:
                image(b, True)
            image(BATCH - 1, False)


def kernel(**inputs):
    import numpy as np
    import concourse.bacc as bacc
    from concourse.bass_utils import run_bass_kernel_spmd as run

    a = {k.replace("L0_conv_", ""): np.asarray(v) for k, v in inputs.items()}

    def per_channel(v):
        return v.reshape(-1, P).T

    k_t, v_t = a["k_w1"].T, a["v_w"].T
    w_proj = np.concatenate([a["q_w1"].T, a["q_w2"].T, k_t[C:], v_t[C:], a["k_w2"].T], 0)
    w_glob = np.concatenate([k_t[:C], v_t[:C]], 0)
    affine = np.concatenate([per_channel(a[n]) for n in
                             ("q_g1", "q_b1", "q_g2", "q_b2", "k_g1", "k_b1", "k_g2", "k_b2", "o_g", "o_b")], 1)
    v_affine = np.stack([np.repeat(a["v_g"][None], P, 0), np.repeat(a["v_b"][None], P, 0)], 1)
    channel = np.arange(P)
    same_group = channel[:, None] // GROUP == channel[None] // GROUP
    arrays = {
        "x": a["x"].reshape(BATCH, NC, P, HW),
        "w_proj": w_proj,
        "w_glob": w_glob,
        "w_out": a["o_w"].T,
        "affine": affine,
        "v_affine": v_affine,
        "ident": np.eye(P, dtype=np.float32),
        "group": np.where(same_group, 1.0 / GROUP, 0.0).astype(np.float32),
    }
    arrays = {f"in_{k}_dram": np.ascontiguousarray(v) for k, v in arrays.items()}
    nc = bacc.Bacc("TRN2", target_bir_lowering=False, num_devices=1)
    args = [nc.dram_tensor(k, v.shape, F32, kind="ExternalInput").ap() for k, v in arrays.items()]
    out = nc.dram_tensor("out_0_dram", (BATCH, NC, P, HW), F32, kind="ExternalOutput").ap()
    build(nc, *args, out)
    r = run(nc, [arrays], core_ids=[0])
    return r.results[0]["out_0_dram"].reshape(BATCH, C, 64, 64)
```

```python
from contextlib import ExitStack

import concourse.bass as bass
from concourse import mybir

F32 = mybir.dt.float32
F32R = mybir.dt.float32r
ALU = mybir.AluOpType
ACT = mybir.ActivationFunctionType
AX = mybir.AxisListType

P = 128
BATCH, C, HW, TC = 2, 512, 4096, 256
GROUP = 16
NC = C // P
NO = TC // P
BLK = 512
NBLK = HW // BLK
TPB = BLK // P
NT = HW // P
NJ = HW // BLK
HELD = 5
CHUNK = 1024
NCH = HW // CHUNK
PAIR = 2 * BLK
NPAIR = HW // PAIR
HALF = BLK // 2
W_COLS = TC // NPAIR
Q_STEPS = NBLK + 1
SCALE = float(TC) ** -0.5
EPS = 1e-5

QG1, QB1, QG2, QB2, KG1, KB1, KG2, KB2, OG, OB = 0, 2, 4, 6, 8, 10, 12, 14, 16, 20
WQ1, WQ2 = 0, 4
WK1, WV, WK2 = 0, 4, 8
NWQ, NWKV = 6, 10
NW = NWQ + NWKV

RING_V, RING_S, RING_T, RING_PT, RING_CTX = 4, 2, 2, 3, 2
START = 8


def build(nc, x, w_proj, w_glob, w_out, affine, v_affine, ident_in, group_in, out):
    with ExitStack() as ctx:
        def sem(name):
            return ctx.enter_context(nc.semaphore(name))

        def sb(name, shape, dt=F32, stack=ctx):
            return stack.enter_context(nc.sbuf_tensor(name, shape, dt))

        aff = sb("aff", [P, 24])
        vaff = sb("vaff", [P, 2, TC])
        ident = sb("ident", [P, P])
        group_mean = sb("group_mean", [P, P])
        bn_part = sb("bn_part", [P, NC, NBLK, 6])
        max_part = sb("max_part", [P, NC, NBLK])
        mean_var = sb("mean_var", [P, NC, 2])
        mean_g = sb("mean_g", [P, NC])
        small = sb("small", [P, 6, NC])
        x_max = sb("x_max", [P, NC])
        rstd = sb("rstd", [P, NC])
        neg_mean = sb("neg_mean", [P, NC])
        e_bias = sb("e_bias", [P, NC])
        e_part = sb("e_part", [P, NC, NPAIR])
        ex_part = sb("ex_part", [P, NC, NPAIR])
        e_sum = sb("e_sum", [P, NC])
        ex_sum = sb("ex_sum", [P, NC])
        g_vec = sb("g_vec", [P, NC])
        k_bias = sb("k_bias", [P, NO])
        v_bias = sb("v_bias", [P, TC])
        blk_max = sb("blk_max", [P, NJ])
        neg_max = sb("neg_max", [P, 2])
        row_sums = sb("row_sums", [P, 2, NCH])
        row_sum = sb("row_sum", [P, 1])
        row_inv = sb("row_inv", [P, 2])

        q_raw = sb("q_raw", [P, 2, NO, P])
        q_hi = sb("q_hi", [P, 2, NO, P], F32R)
        q_lo = sb("q_lo", [P, 2, NO, P], F32R)
        x_res = sb("x_res", [P, 2, BLK])

        with ExitStack() as region:
            x_img = sb("x_img", [P, NC, HW], stack=region)
            w_raw = sb("w_raw", [P, NW, TC], stack=region)
            wq_hi = sb("wq_hi", [P, NWQ, TC], F32R, region)
            wq_lo = sb("wq_lo", [P, NWQ, TC], F32R, region)
            e_img = sb("e_img", [P, 2, PAIR], stack=region)
            wg_raw = sb("wg_raw", [P, 2 * NC, TC], stack=region)
            g_wide = sb("g_wide", [P, NC, P], stack=region)
            x_hi_odd = sb("x_hi_odd", [P, NC, BLK], F32R, region)
            x_lo_odd = sb("x_lo_odd", [P, NC, BLK], F32R, region)
        WEIGHTS_END = (NW + 2 * NWQ) * TC // (2 * TC)
        k_hi = sb("k_hi", [P, NO, HW], F32R)
        k_lo = sb("k_lo", [P, NO, HW], F32R)
        v_hl = sb("v_hl", [P, NT, 2 * TC], F32R)

        with ExitStack() as region:
            x_blk = sb("x_blk", [P, NC, BLK], F32, region)
            x_hi = sb("x_hi", [P, NC, BLK], F32R, region)
            x_lo = sb("x_lo", [P, NC, BLK], F32R, region)
            w_hi = sb("w_hi", [P, NWKV, TC], F32R, region)
            w_lo = sb("w_lo", [P, NWKV, TC], F32R, region)
            h_hi = sb("h_hi", [P, NO, BLK], F32R, region)
            h_lo = sb("h_lo", [P, NO, BLK], F32R, region)
            lin = sb("lin", [P, 2 * NO, BLK], F32, region)
            v_tmp = sb("v_tmp", [P, 2, TC], F32, region)
        scores = sb("scores", [P, HW])
        probs = sb("probs", [P, 2, CHUNK])
        pt_hi = sb("pt_hi", [P, RING_PT, BLK], F32R)
        pt_lo = sb("pt_lo", [P, RING_PT, BLK], F32R)
        ct_hi = sb("ct_hi", [P, NO, BLK], F32R)
        ct_lo = sb("ct_lo", [P, NO, BLK], F32R)
        wo_hi = sb("wo_hi", [P, NO, C], F32R)
        wo_lo = sb("wo_lo", [P, NO, C], F32R)
        ctx_part = sb("ctx_part", [P, TC])
        ctx_row = sb("ctx_row", [P, TC])
        y_out = sb("y_out", [P, NC, BLK])

        q_dram = nc.dram_tensor("q_scratch", (BATCH, NO, P, HW), F32, kind="Internal").ap()

        ps = ctx.enter_context(nc.psum_tensor("ps", [P, 8, BLK], F32))
        S_BANK, T_BANK, CTX_BANK, CT_BANK, O_BANK, V_BANK = 0, 2, 4, 6, 7, 4

        const_in = sem("const_in")
        img_in = [sem(f"img_in{s}") for s in range(NBLK)]
        img_ready = sem("img_ready")
        wq_in, wkv_in, wg_in, wo_in = sem("wq_in"), sem("wkv_in"), sem("wg_in"), sem("wo_in")
        wq_hi_done, wq_split, wkv_hi_done, wkv_split = (
            sem("wq_hi_done"), sem("wq_split"), sem("wkv_hi_done"), sem("wkv_split"))
        wo_hi_done, wo_split = sem("wo_hi_done"), sem("wo_split")
        first_stats, first_max, x_max_done = sem("first_stats"), sem("first_max"), sem("x_max_done")
        glob_step, wv_scaled = sem("glob_step"), sem("wv_scaled")
        stat_step = sem("stat_step")
        piece_in, piece_read = sem("piece_in"), sem("piece_read")
        mean_ready, var_ready = sem("mean_ready"), sem("var_ready")
        stat_mean, stat_var, ve_ready, sqrt_done = (
            sem("stat_mean"), sem("stat_var"), sem("ve_ready"), sem("sqrt_done"))
        coef_ready, e_bias_ready, e_done, ex_done, g_ready, glob_ready, glob_done = (
            sem("coef_ready"), sem("e_bias_ready"), sem("e_done"), sem("ex_done"), sem("g_ready"),
            sem("glob_ready"), sem("glob_done"))
        x_in = [sem("x_in0"), sem("x_in1")]
        x_arrived = sem("x_arrived")
        xq_norm, xkv_norm, xh_ready, xl_ready = sem("xq_norm"), sem("xkv_norm"), sem("xh_ready"), sem("xl_ready")
        q1_ready, q2_ready, k1_ready, k2_ready = sem("q1_ready"), sem("q2_ready"), sem("k1_ready"), sem("k2_ready")
        q1_out, q2_out, k1_out, k2_out = sem("q1_out"), sem("q2_out"), sem("k1_out"), sem("k2_out")
        h_hi_done, h_split, k_hi_done, k_split = sem("h_hi_done"), sem("h_split"), sem("k_hi_done"), sem("k_split")
        v_ready, v_read, v_hi_done, v_split = (
            sem("v_ready"), sem("v_read"), sem("v_hi_done"), sem("v_split"))
        q_stored = sem("q_stored")
        q_in = [sem("q_in0"), sem("q_in1")]
        q_hi_done, q_split = sem("q_hi_done"), sem("q_split")
        scores_ready, scores_copied, max_ready, probs_ready = (
            sem("scores_ready"), sem("scores_copied"), sem("max_ready"), sem("probs_ready"))
        tposed, pt_hi_done, pt_split, pv_done = sem("tposed"), sem("pt_hi_done"), sem("pt_split"), sem("pv_done")
        sum_done, inv_ready, part_ready, ctx_ready = (
            sem("sum_done"), sem("inv_ready"), sem("part_ready"), sem("ctx_ready"))
        ct_ready, ct_hi_done, ct_split = sem("ct_ready"), sem("ct_hi_done"), sem("ct_split")
        o_ready, o_relu, y_ready = sem("o_ready"), sem("o_relu"), sem("y_ready")
        x_res_in = [sem("x_res_in0"), sem("x_res_in1")]
        y_stored = [sem(f"y_stored{s}") for s in range(NC)]

        block = ctx.enter_context(nc.Block())

        def key_cols(j):
            return slice(j * BLK, (j + 1) * BLK)

        HALVES = (slice(0, HALF), slice(HALF, BLK))

        def q_half(b, n, h):
            return b * (4 * NBLK) + n * 2 + h

        def kv_half(b, blk, h):
            return b * (4 * NBLK) + 2 * NBLK + blk * 2 + h

        def results(b, n, oc):
            return b * (NBLK * NO) + n * NO + oc

        @block.gpsimd
        def _(pool):
            for s in (xl_ready, q1_ready, q2_ready, q1_out, q2_out, h_split, k_split, v_read, v_split,
                      q_stored, scores_ready, scores_copied, max_ready, probs_ready, tposed, pt_split,
                      pv_done, inv_ready, part_ready, ctx_ready, ct_ready, ct_split, o_ready, o_relu, y_ready,
                      piece_read, e_done, ex_done, k1_out, k2_out,
                      *y_stored):
                pool.sem_inc(s, START)

            def add_residual(g, co):
                pool.wait_ge(o_relu, START + g * NC + co + 1)
                pool.wait_ge(x_res_in[co % 2], g * (16 * NC // 2) + 16 * (co // 2) + 16)
                nc.gpsimd.tensor_tensor(y_out[:, co], y_out[:, co], x_res[:, co % 2], ALU.add)\
                    .then_inc(y_ready, 1)

            def normalise(b, blk, h):
                pool.wait_ge(x_in[h], b * (16 * (NBLK - 1)) + blk * 16)
                pool.sem_inc(x_arrived, 1)
                cols = slice(h * HALF, (h + 1) * HALF)
                for c in range(NC):
                    last = nc.gpsimd.tensor_scalar(x_blk[:, c, cols], x_blk[:, c, cols], neg_mean[:, c:c + 1],
                                                   rstd[:, c:c + 1], ALU.add, ALU.mult)
                last.then_inc(xkv_norm, 1)

            def h_low(b, n):
                for oc in range(NO):
                    pool.wait_ge(h_hi_done, 2 * results(b, 0, 0) + n * NO + oc + 1)
                    nc.gpsimd.tensor_tensor(h_lo[:, oc], lin[:, oc], h_hi[:, oc].bitcast(F32), ALU.subtract)\
                        .then_inc(h_split, 1)

            def q_weights_low(b):
                pool.wait_ge(wq_hi_done, b + 1)
                nc.gpsimd.tensor_tensor(wq_lo[:], w_raw[:, 0:NWQ], wq_hi[:].bitcast(F32), ALU.subtract)\
                    .then_inc(wq_split, 1)

            def scale_values_weights(b, pair):
                pool.wait_ge(wkv_in, b * 16 + 16)
                cols = bass.ds(pair * W_COLS, W_COLS)
                weights = w_raw[:, NWQ + WV:NWQ + WV + NC, cols]
                nc.gpsimd.tensor_tensor(weights, weights, vaff[:, 0:1, cols].broadcast_to([P, NC, W_COLS]), ALU.mult)\
                    .then_inc(wv_scaled, 1)

            def kv_weights_low(b, pair):
                cols = bass.ds(pair * W_COLS, W_COLS)
                pool.wait_ge(wkv_hi_done, b * NPAIR + pair + 1)
                nc.gpsimd.tensor_tensor(w_lo[:, :, cols], w_raw[:, NWQ:, cols], w_hi[:, :, cols].bitcast(F32),
                                        ALU.subtract).then_inc(wkv_split, 1)

            def image(b, more_images):
                h_low(b, 0)
                with pool.Fori(1, NPAIR) as pair:
                    h_low(b, pair * 2 - 1)
                    scale_values_weights(b, pair - 1)
                    h_low(b, pair * 2)
                    kv_weights_low(b, pair - 1)
                scale_values_weights(b, NPAIR - 1)
                kv_weights_low(b, NPAIR - 1)
                with pool.Fori(0, NBLK - 1) as blk:
                    for h in range(2):
                        normalise(b, blk + 1, h)
                    h_low(b, blk + NBLK)
                h_low(b, 2 * NBLK - 1)
                pool.wait_ge(wo_hi_done, b + 1)
                nc.gpsimd.tensor_tensor(wo_lo[:], x_res[:], wo_hi[:].bitcast(F32), ALU.subtract).then_inc(wo_split, 1)
                with pool.Fori(0, NBLK - 1) as blk:
                    for co in range(NC):
                        add_residual(b * NBLK + blk, co)
                if more_images:
                    q_weights_low(b + 1)
                for co in range(NC):
                    add_residual(b * NBLK + (NBLK - 1), co)

            pool.wait_ge(const_in, 64)
            q_weights_low(0)
            with pool.Fori(0, BATCH - 1) as b:
                image(b, True)
            image(BATCH - 1, False)

        @block.sync
        def _(sp):
            def load_block(b, n):
                sp.dma_start(x_img[:, :, key_cols(n)], x[bass.ds(b, 1), :, :, key_cols(n)]
                             .rearrange("b c p n -> p (b c) n")).then_inc(img_in[n], 16)

            def load_weights(rows, done):
                sp.dma_start(w_raw[:, rows], w_proj.rearrange("(r p) o -> p r o", p=P)[:, rows]).then_inc(done, 16)

            def load_q_weights(b):
                sp.wait_ge(pv_done, START + b * (NT * NJ) - (NJ - -(-WEIGHTS_END // TPB)))
                load_weights(slice(0, NWQ), wq_in)
                load_block(b, 2)
                load_block(b, 3)

            def load_rest(b):
                sp.wait_ge(pv_done, START + b * (NT * NJ))
                load_weights(slice(NWQ, NW), wkv_in)
                for n in range(4, NBLK):
                    load_block(b, n)
                sp.dma_start(wg_raw[:], w_glob.rearrange("(r p) o -> p r o", p=P)).then_inc(wg_in, 16)

            def arrived(b, blocks):
                for n in blocks:
                    sp.wait_ge(img_in[n], b * 16 + 16)
                    sp.sem_inc(img_ready, 1)

            def load_half(b, blk, h):
                sp.dma_start(x_blk[:, :, h * HALF:(h + 1) * HALF],
                             x[bass.ds(b, 1), :, :, bass.ds(blk * BLK + h * HALF, HALF)]
                             .rearrange("b c p n -> p (b c) n")).then_inc(x_in[h], 16)

            def load_next_x(b, blk):
                for h in range(2):
                    sp.wait_ge(xl_ready, START + kv_half(b, blk, h) + 1)
                    load_half(b, blk + 1, h)

            def store_q(b, n):
                for oc in range(NO):
                    sp.wait_ge(q2_out, START + results(b, n, oc) + 1)
                    sp.dma_start(q_dram[bass.ds(b, 1), oc, :, bass.ds(n * BLK, BLK)]
                                 .rearrange("b p n -> p (b n)"), lin[:, NO + oc, :]).then_inc(q_stored, 16)

            def load_q(b, tile, slot):
                sp.dma_start(q_raw[:, slot], q_dram[bass.ds(b, 1), :, :, bass.ds(tile * P, P)]
                             .rearrange("b o p n -> p (b o) n")).then_inc(q_in[slot], 16)

            def load_res(b, blk, co):
                sp.dma_start(x_res[:, co % 2], x[bass.ds(b, 1), co, :, bass.ds(blk * BLK, BLK)]
                             .rearrange("b p n -> p (b n)")).then_inc(x_res_in[co % 2], 16)

            def load_piece(b, blk, c):
                sp.dma_start(x_res[:, 0], x[1:][bass.ds(b, 1), c, :, bass.ds(blk * BLK, BLK)]
                             .rearrange("b p n -> p (b n)")).then_inc(piece_in, 16)

            def attend(b, blk, last, more_images):
                t0 = (b * NBLK + blk) * TPB
                y0 = (b * NBLK + blk) * NC
                sp.wait_ge(wo_split, b + 1)
                for i in range(TPB):
                    if more_images:
                        sp.wait_ge(piece_read, START + t0 + i)
                        load_piece(b, blk, i)
                    if not last or i < TPB - 2:
                        sp.wait_ge(q_split, t0 + i + 1)
                        load_q(b, blk * TPB + i + 2, i % 2)
                if more_images:
                    if last:
                        sp.wait_ge(scores_copied, START + (b + 1) * (NT * NJ))
                        load_block(b + 1, 0)
                        load_block(b + 1, 1)
                    sp.wait_ge(piece_read, START + t0 + TPB)
                load_res(b, blk, 1)
                load_res(b, blk, 0)
                if last and more_images:
                    load_q_weights(b + 1)
                    arrived(b + 1, range(0, 2))
                for co in range(NC):
                    sp.wait_ge(y_ready, START + y0 + co + 1)
                    sp.dma_start(out[bass.ds(b, 1), co, :, bass.ds(blk * BLK, BLK)]
                                 .rearrange("b p n -> p (b n)"), y_out[:, co])\
                        .then_inc(y_stored[co], 16)
                    if co + 2 < NC:
                        load_res(b, blk, co + 2)
                    if last and more_images and co == 1:
                        arrived(b + 1, range(2, 4))
                if last and more_images:
                    load_rest(b + 1)

            def image(b, more_images):
                arrived(b, range(4, NBLK))
                with sp.Fori(0, NPAIR - 1) as pair:
                    for odd in range(2):
                        store_q(b, pair * 2 + odd)
                store_q(b, NBLK - 2)
                load_next_x(b, 0)
                store_q(b, NBLK - 1)
                with sp.Fori(1, NBLK - 1) as blk:
                    load_next_x(b, blk)
                sp.wait_ge(q_stored, START + (b + 1) * (16 * NO * NBLK))
                sp.dma_start(x_res[:], w_out.rearrange("(r p) o -> p r o", p=P)).then_inc(wo_in, 16)
                load_q(b, 0, 0)
                load_q(b, 1, 1)
                with sp.Fori(0, NBLK - 1) as blk:
                    attend(b, blk, False, more_images)
                attend(b, NBLK - 1, True, more_images)

            for n in range(NBLK):
                load_block(0, n)
            sp.dma_start(aff[:], affine).then_inc(const_in, 16)
            sp.dma_start(vaff[:], v_affine).then_inc(const_in, 16)
            sp.dma_start(ident[:], ident_in).then_inc(const_in, 16)
            sp.dma_start(group_mean[:], group_in).then_inc(const_in, 16)
            load_weights(slice(0, NWQ), wq_in)
            load_weights(slice(NWQ, NW), wkv_in)
            sp.dma_start(wg_raw[:], w_glob.rearrange("(r p) o -> p r o", p=P)).then_inc(wg_in, 16)
            arrived(0, range(0, 4))
            with sp.Fori(0, BATCH - 1) as b:
                image(b, True)
            image(BATCH - 1, False)
            for s in range(NC):
                sp.wait_ge(y_stored[s], START + BATCH * 16 * NBLK)
            sp.wait_ge(q_stored, START + BATCH * 16 * NO * NBLK)

        @block.scalar
        def _(act):
            def q_weights_high(b):
                act.wait_ge(wq_in, b * 16 + 16)
                nc.scalar.copy(wq_hi[:], w_raw[:, 0:NWQ]).then_inc(wq_hi_done, 1)

            def deviation(b):
                act.wait_ge(ve_ready, b + 1)
                nc.scalar.activation(small[:, 1], small[:, 0], ACT.Sqrt).then_inc(sqrt_done, 1)

            def x_high_block(b, n, hi, parts=(slice(0, BLK),)):
                act.wait_ge(xq_norm, b * Q_STEPS + n + 1)
                act.wait_ge(q1_ready, START + results(b, n, 0) - 2 * NO)
                for part in parts:
                    nc.scalar.copy(hi[:, :, part], x_blk[:, :, part]).then_inc(xh_ready, 2 // len(parts))

            def x_high_half(b, blk, h):
                act.wait_ge(xkv_norm, b * (2 * (NBLK - 1)) + 2 * (blk - 1) + h + 1)
                act.wait_ge(v_ready, (b * NBLK + blk) * TPB - TPB + 2 * (h + 1))
                cols = slice(h * HALF, (h + 1) * HALF)
                nc.scalar.copy(x_hi[:, :, cols], x_blk[:, :, cols]).then_inc(xh_ready, 1)

            def relu(bank, ready, out_sem, count, gain, bias):
                act.wait_ge(ready, count)
                nc.scalar.activation(lin[:, bank], ps[:, bank], ACT.Relu, bias=bias, scale=gain).then_inc(out_sem, 1)

            def finish_q1(b, n):
                act.wait_ge(h_split, START + 2 * results(b, 0, 0) + n * NO)
                for oc in range(NO):
                    relu(oc, q1_ready, q1_out, START + results(b, n, oc) + 1, aff[:, QG1 + oc:QG1 + oc + 1],
                         aff[:, QB1 + oc:QB1 + oc + 1])

            def finish_q2(b, n):
                act.wait_ge(q_stored, START + 16 * results(b, n, 0))
                for oc in range(NO):
                    relu(NO + oc, q2_ready, q2_out, START + results(b, n, oc) + 1, aff[:, QG2 + oc:QG2 + oc + 1],
                         aff[:, QB2 + oc:QB2 + oc + 1])

            def finish_k1(b, n):
                for oc in range(NO):
                    relu(oc, k1_ready, k1_out, results(b, n, oc) + 1, aff[:, KG1 + oc:KG1 + oc + 1],
                         k_bias[:, oc:oc + 1])

            def finish_k2(b, n):
                act.wait_ge(q_stored, START + b * (16 * NO * NBLK) + 16 * NO * NBLK)
                act.wait_ge(k_split, START + results(b, n, 0))
                for oc in range(NO):
                    relu(NO + oc, k2_ready, k2_out, results(b, n, oc) + 1, aff[:, KG2 + oc:KG2 + oc + 1],
                         aff[:, KB2 + oc:KB2 + oc + 1])

            def global_exp(b, pair, chunks):
                for c in chunks:
                    act.wait_ge(ex_done, START + (b * NPAIR + pair) * NC + c - 1)
                    nc.scalar.activation(e_img[:, c % 2], x_img[:, c, bass.ds(pair * PAIR, PAIR)], ACT.Exp,
                                         bias=e_bias[:, c:c + 1], scale=rstd[:, c:c + 1],
                                         accum_out=e_part[:, c, bass.ds(pair, 1)]).then_inc(e_done, 1)

            def kv_weights_high(b, pair):
                act.wait_ge(wv_scaled, b * NPAIR + pair + 1)
                cols = bass.ds(pair * W_COLS, W_COLS)
                nc.scalar.copy(w_hi[:, :, cols], w_raw[:, NWQ:, cols]).then_inc(wkv_hi_done, 1)

            def kv_block(b, blk, last):
                finish_k1(b, blk)
                if last:
                    q_high(0, b * (NT // 2), b * (NJ * NT))
                    q_high(1, b * (NT // 2), b * (NJ * NT))
                else:
                    for h in range(2):
                        x_high_half(b, blk + 1, h)
                finish_k2(b, blk)

            def q_high(slot, pair, scored):
                act.wait_ge(q_in[slot], pair * 16 + 16)
                act.wait_ge(scores_ready, START + scored)
                nc.scalar.copy(q_hi[:, slot], q_raw[:, slot]).then_inc(q_hi_done, 1)

            def exponential(t, parity, c):
                if c == 0:
                    act.wait_ge(max_ready, START + t + 1)
                    act.wait_ge(inv_ready, START + t - 1)
                act.wait_ge(tposed, START + t * (2 * NCH) + 2 * c - 2)
                nc.scalar.activation(probs[:, c % 2], scores[:, c * CHUNK:(c + 1) * CHUNK], ACT.Exp,
                                     bias=neg_max[:, parity:parity + 1],
                                     accum_out=row_sums[:, parity, c:c + 1]).then_inc(probs_ready, 1)

            def pt_high(t, j):
                act.wait_ge(tposed, START + t * NJ + j + 1)
                act.wait_ge(pv_done, START + t * NJ + j + 1 - (2 if j < 2 else RING_PT))
                nc.scalar.copy(pt_hi[:, j % RING_PT], ps[:, T_BANK + j % RING_T]).then_inc(pt_hi_done, 1)

            def ctx_part_out(t, parity):
                act.wait_ge(pv_done, START + t * NJ + NJ)
                act.wait_ge(inv_ready, START + t + 1)
                act.wait_ge(ctx_ready, START + t)
                nc.scalar.activation(ctx_part[:], ps[:, CTX_BANK + parity, TC:2 * TC], ACT.Copy,
                                     scale=row_inv[:, parity:parity + 1]).then_inc(part_ready, 1)

            def ct_high(t, y0, i):
                act.wait_ge(ct_ready, START + t + 1)
                if i == 0:
                    act.wait_ge(o_ready, START + y0)
                nc.scalar.copy(ct_hi[:, :, i * P:(i + 1) * P], ps[:, CT_BANK, 0:TC].rearrange("p (o n) -> p o n", o=NO))\
                    .then_inc(ct_hi_done, 1)

            def project_out(g, co):
                act.wait_ge(o_ready, START + g * NC + co + 1)
                act.wait_ge(y_stored[co], START + g * 16)
                nc.scalar.activation(y_out[:, co], ps[:, O_BANK - co % 2], ACT.Relu,
                                     bias=aff[:, OB + co:OB + co + 1], scale=aff[:, OG + co:OG + co + 1])\
                    .then_inc(o_relu, 1)

            def attend(b, blk, last, more_images):
                g = b * NBLK + blk
                for i in range(TPB):
                    t = g * TPB + i
                    more = not last or i < TPB - 1
                    for j in range(NJ):
                        pt_high(t, j)
                        if j in (1, 3):
                            exponential(t, i % 2, 2 + j // 2)
                        if i > 0 and j == 2:
                            ctx_part_out(t - 1, (i - 1) % 2)
                        if i > 0 and j == 4:
                            ct_high(t - 1, g * NC, i - 1)
                        if j == 5 and (not last or i < TPB - 2):
                            q_high(i % 2, g * (TPB // 2) + i // 2 + 1, t * NJ + NJ)
                    if i == TPB - 1:
                        if last and more_images:
                            q_weights_high(b + 1)
                            deviation(b + 1)
                        ctx_part_out(t, i % 2)
                        ct_high(t, g * NC, i)
                        project_out(g, 0)
                        if last and more_images:
                            x_high_block(b + 1, 0, x_hi, HALVES)
                        project_out(g, 1)
                    if more:
                        exponential(t + 1, (i + 1) % 2, 0)
                        exponential(t + 1, (i + 1) % 2, 1)
                project_out(g, 2)
                project_out(g, 3)
                if last and more_images:
                    x_high_block(b + 1, 1, x_hi_odd)

            def image(b, more_images):
                act.wait_ge(y_stored[0], START + b * (16 * NBLK))
                finish_q1(b, 0)
                act.wait_ge(e_bias_ready, b + 1)
                act.wait_ge(img_ready, b * NBLK + 2)
                for s in range(1, NC):
                    act.wait_ge(y_stored[s], START + b * (16 * NBLK))
                global_exp(b, 0, (0, 1))
                with act.Fori(1, NPAIR) as pair:
                    n = pair * 2
                    x_high_block(b, n, x_hi)
                    global_exp(b, pair - 1, (2,))
                    finish_q1(b, n - 1)
                    global_exp(b, pair - 1, (3,))
                    finish_q2(b, n - 2)
                    x_high_block(b, n + 1, x_hi_odd)
                    act.wait_ge(img_ready, b * NBLK + pair * 2 + 2)
                    global_exp(b, pair, (0,))
                    finish_q1(b, n)
                    global_exp(b, pair, (1,))
                    finish_q2(b, n - 1)
                    kv_weights_high(b, pair - 1)
                x_high_block(b, NBLK, x_hi)
                kv_weights_high(b, NPAIR - 1)
                finish_q1(b, NBLK - 1)
                global_exp(b, NPAIR - 1, (2, 3))
                finish_q2(b, NBLK - 2)
                finish_q2(b, NBLK - 1)
                act.wait_ge(glob_done, b + 1)
                with act.Fori(0, NBLK - 1) as blk:
                    kv_block(b, blk, False)
                kv_block(b, NBLK - 1, True)
                act.wait_ge(wo_in, b * 16 + 16)
                nc.scalar.copy(wo_hi[:], x_res[:]).then_inc(wo_hi_done, 1)
                exponential(b * NT, 0, 0)
                exponential(b * NT, 0, 1)
                with act.Fori(0, NBLK - 1) as blk:
                    attend(b, blk, False, more_images)
                attend(b, NBLK - 1, True, more_images)

            act.wait_ge(const_in, 64)
            deviation(0)
            q_weights_high(0)
            x_high_block(0, 0, x_hi, HALVES)
            x_high_block(0, 1, x_hi_odd)
            with act.Fori(0, BATCH - 1) as b:
                image(b, True)
            image(BATCH - 1, False)

        @block.tensor
        def _(pe):
            def three(out_ap, terms, done):
                n = len(terms)
                for k, (w, m) in enumerate(terms):
                    last = nc.tensor.matmul(out_ap, w, m, start=(k == 0), stop=(k == n - 1))
                last.then_inc(done, 1)

            def linear(bank, w_hi, w_lo, row, chunks, oc, hi, lo, done):
                cols = slice(oc * P, (oc + 1) * P)
                terms = []
                for c in range(chunks):
                    terms += [(w_hi[:, row + c, cols], hi[:, c]), (w_lo[:, row + c, cols], hi[:, c]),
                              (w_hi[:, row + c, cols], lo[:, c])]
                three(ps[:, bank], terms, done)

            def q1(b, n, hi, lo):
                pe.wait_ge(xl_ready, START + q_half(b, n, 1) + 1)
                for oc in range(NO):
                    pe.wait_ge(q1_out, START + results(b, n, oc) + 1 - NO)
                    linear(oc, wq_hi, wq_lo, WQ1, NC, oc, hi, lo, q1_ready)

            def q2(b, n):
                pe.wait_ge(h_split, START + 2 * results(b, 0, 0) + n * NO + NO)
                for oc in range(NO):
                    pe.wait_ge(q2_out, START + results(b, n, oc) + 1 - NO)
                    linear(NO + oc, wq_hi, wq_lo, WQ2, NO, oc, h_hi, h_lo, q2_ready)

            def k1(b, blk, first):
                pe.wait_ge(xl_ready, START + kv_half(b, blk, 1) + 1)
                for oc in range(NO):
                    if first:
                        pe.wait_ge(q1_out, START + results(b, NBLK - 1, oc) + 1)
                    else:
                        pe.wait_ge(k1_out, START + results(b, blk, oc) + 1 - NO)
                    linear(oc, w_hi, w_lo, WK1, NC, oc, x_hi, x_lo, k1_ready)

            def values_k2(b, blk):
                for u in range(TPB):
                    if u == 2:
                        pe.wait_ge(glob_done, b + 1)
                    values(b * NBLK + blk, u)
                pe.wait_ge(h_split, START + 2 * results(b, 0, 0) + NBLK * NO + blk * NO + NO)
                for oc in range(NO):
                    pe.wait_ge(k2_out, START + results(b, blk, oc) + 1 - NO)
                    linear(NO + oc, w_hi, w_lo, WK2, NO, oc, h_hi, h_lo, k2_ready)

            def values(g, u):
                pe.wait_ge(v_read, START + g * TPB + u + 1 - RING_V)
                cols = slice(u * P, (u + 1) * P)
                terms = []
                for c in range(NC):
                    terms += [(x_hi[:, c, cols], w_hi[:, WV + c]), (x_hi[:, c, cols], w_lo[:, WV + c]),
                              (x_lo[:, c, cols], w_hi[:, WV + c])]
                three(ps[:, V_BANK + u % RING_V, 0:TC], terms, v_ready)

            def score(t, slot, j):
                pe.wait_ge(scores_copied, START + t * NJ + j + 1 - RING_S)
                terms = []
                for c in range(NO):
                    terms += [(q_hi[:, slot, c], k_hi[:, c, key_cols(j)]), (q_hi[:, slot, c], k_lo[:, c, key_cols(j)]),
                              (q_lo[:, slot, c], k_hi[:, c, key_cols(j)])]
                three(ps[:, S_BANK + j % RING_S], terms, scores_ready)

            def turn(t, j):
                if j % 2 == 0:
                    pe.wait_ge(probs_ready, START + t * NCH + j // 2 + 1)
                pe.wait_ge(pt_split, START + t * NJ + j + 1 - RING_T)
                for k in range(BLK // P):
                    at = (j % 2) * BLK + k * P
                    last = nc.tensor.transpose(ps[:, T_BANK + j % RING_T, k * P:(k + 1) * P],
                                               probs[:, (j // 2) % 2, at:at + P], ident[:])
                last.then_inc(tposed, 1)

            def context(t, parity, j):
                if j == 0:
                    pe.wait_ge(ctx_ready, START + t + 1 - RING_CTX)
                pe.wait_ge(pt_split, START + t * NJ + j + 1)
                bank = ps[:, CTX_BANK + parity]
                for k in range(BLK // P):
                    m = j * (BLK // P) + k
                    cols = slice(k * P, (k + 1) * P)
                    nc.tensor.matmul(bank, pt_hi[:, j % RING_PT, cols], v_hl[:, m], start=(m == 0), stop=False)
                    last = nc.tensor.matmul(bank[:, 0:TC], pt_lo[:, j % RING_PT, cols], v_hl[:, m, 0:TC],
                                            start=False, stop=(m == NT - 1))
                last.then_inc(pv_done, 1)

            def turn_context(t, y0, i):
                pe.wait_ge(ctx_ready, START + t + 1)
                pe.wait_ge(ct_split, START + t)
                if i == 0:
                    pe.wait_ge(o_relu, START + y0)
                for c in range(NO):
                    last = nc.tensor.transpose(ps[:, CT_BANK, c * P:(c + 1) * P], ctx_row[:, c * P:(c + 1) * P], ident[:])
                last.then_inc(ct_ready, 1)

            def project_out(g, co):
                if co == 0:
                    pe.wait_ge(ct_split, START + g * TPB + TPB)
                pe.wait_ge(o_relu, START + g * NC + (co - 1 if co >= 2 else 0))
                cols = slice(co * P, (co + 1) * P)
                terms = []
                for c in range(NO):
                    terms += [(wo_hi[:, c, cols], ct_hi[:, c]), (wo_lo[:, c, cols], ct_hi[:, c]),
                              (wo_hi[:, c, cols], ct_lo[:, c])]
                three(ps[:, O_BANK - co % 2], terms, o_ready)

            def attend(b, blk, last, more_images):
                g = b * NBLK + blk
                for i in range(TPB):
                    t = g * TPB + i
                    more = not last or i < TPB - 1
                    own = i == TPB - 1
                    if more:
                        pe.wait_ge(q_split, t + 2)
                    for j in range(NJ - 1):
                        if more and not (own and j >= HELD):
                            score(t + 1, (i + 1) % 2, j)
                        turn(t, j)
                        if own and j == NJ - 2:
                            turn(t, NJ - 1)
                        if j > 0:
                            context(t, i % 2, j - 1)
                        if i > 0 and j == 3:
                            turn_context(t - 1, g * NC, i - 1)
                        if own and last and more_images and j == 4:
                            group_means(b + 1)
                        if own and last and more_images and j == 5:
                            group_variances(b + 1)
                    if not own:
                        turn(t, NJ - 1)
                        if more:
                            score(t + 1, (i + 1) % 2, NJ - 1)
                    context(t, i % 2, NJ - 2)
                    context(t, i % 2, NJ - 1)
                    if own:
                        if more:
                            score(t + 1, (i + 1) % 2, HELD)
                        turn_context(t, g * NC, i)
                        if more:
                            for j in range(HELD + 1, NJ):
                                score(t + 1, (i + 1) % 2, j)
                        for co in range(NC):
                            project_out(g, co)

            def group_means(b):
                pe.wait_ge(stat_mean, b + 1)
                pe.wait_ge(scores_copied, START + b * (NT * NJ))
                nc.tensor.matmul(ps[:, S_BANK, 0:NC], group_mean[:], small[:, 2], start=True, stop=True)\
                    .then_inc(mean_ready, 1)

            def group_variances(b):
                pe.wait_ge(stat_var, b + 1)
                nc.tensor.matmul(ps[:, S_BANK, 0:NC], group_mean[:], small[:, 3], start=True, stop=True)\
                    .then_inc(var_ready, 1)

            def image(b, more_images):
                pe.wait_ge(wq_split, b + 1)
                q1(b, 0, x_hi, x_lo)
                q1(b, 1, x_hi_odd, x_lo_odd)
                q2(b, 0)
                with pe.Fori(1, NPAIR) as pair:
                    n = pair * 2
                    q1(b, n, x_hi, x_lo)
                    q2(b, n - 1)
                    q1(b, n + 1, x_hi_odd, x_lo_odd)
                    q2(b, n)
                pe.wait_ge(wkv_split, (b + 1) * NPAIR)
                k1(b, 0, True)
                q2(b, NBLK - 1)
                pe.wait_ge(g_ready, b + 1)
                pe.wait_ge(wg_in, b * 16 + 16)
                for oc in range(NO):
                    for c in range(NC):
                        nc.tensor.matmul(ps[:, 7, 8 + oc:9 + oc], wg_raw[:, c, oc * P:(oc + 1) * P], g_vec[:, c:c + 1],
                                         start=(c == 0), stop=(c == NC - 1))
                for c in range(NC):
                    last = nc.tensor.matmul(ps[:, 6, 0:TC], g_wide[:, c], wg_raw[:, NC + c], start=(c == 0),
                                            stop=(c == NC - 1))
                last.then_inc(glob_ready, 1)
                with pe.Fori(0, NBLK - 1) as blk:
                    values_k2(b, blk)
                    k1(b, blk + 1, False)
                values_k2(b, NBLK - 1)
                pe.wait_ge(q_split, b * NT + 1)
                for j in range(NJ):
                    if j == 0 or j == NJ - 1:
                        pe.wait_ge(k_split, START + results(b, NBLK - 1 + (j == NJ - 1), 0))
                    score(b * NT, 0, j)
                with pe.Fori(0, NBLK - 1) as blk:
                    attend(b, blk, False, more_images)
                attend(b, NBLK - 1, True, more_images)

            pe.wait_ge(const_in, 64)
            group_means(0)
            group_variances(0)
            with pe.Fori(0, BATCH - 1) as b:
                image(b, True)
            image(BATCH - 1, False)

        @block.vector
        def _(dve):
            def x_normalise(b, n, source):
                dve.wait_ge(xl_ready, START + q_half(b, n, 0))
                for c in range(NC):
                    last = nc.vector.tensor_scalar(x_blk[:, c], source(c), neg_mean[:, c:c + 1], rstd[:, c:c + 1],
                                                   ALU.add, ALU.mult)
                last.then_inc(xq_norm, 1)

            def x_low_block(b, n, hi, lo, parts=(slice(0, BLK),)):
                for k, part in enumerate(parts):
                    dve.wait_ge(xh_ready, q_half(b, n, 0) + 2 * (k + 1) // len(parts))
                    nc.vector.tensor_tensor(lo[:, :, part], x_blk[:, :, part], hi[:, :, part].bitcast(F32),
                                            ALU.subtract).then_inc(xl_ready, 2 // len(parts))

            def x_low_half(b, blk, h):
                dve.wait_ge(xh_ready, kv_half(b, blk, h) + 1)
                cols = slice(h * HALF, (h + 1) * HALF)
                nc.vector.tensor_tensor(x_lo[:, :, cols], x_blk[:, :, cols], x_hi[:, :, cols].bitcast(F32),
                                        ALU.subtract).then_inc(xl_ready, 1)

            def q1_high(b, n):
                dve.wait_ge(q2_ready, START + results(b, n, 0))
                for oc in range(NO):
                    dve.wait_ge(q1_out, START + results(b, n, oc) + 1)
                    nc.vector.tensor_copy(h_hi[:, oc], lin[:, oc]).then_inc(h_hi_done, 1)

            def q1_low(b, n):
                for oc in range(NO):
                    dve.wait_ge(h_hi_done, 2 * results(b, 0, 0) + n * NO + oc + 1)
                    nc.vector.tensor_tensor(h_lo[:, oc], lin[:, oc], h_hi[:, oc].bitcast(F32), ALU.subtract)\
                        .then_inc(h_split, 1)

            def k1_high(b, blk):
                for oc in range(NO):
                    dve.wait_ge(k1_out, START + results(b, blk, oc) + 1)
                    nc.vector.tensor_copy(h_hi[:, oc], lin[:, oc]).then_inc(h_hi_done, 1)

            def split_k(b, blk, oc):
                cols = bass.ds(blk * BLK, BLK)
                dve.wait_ge(k2_out, START + results(b, blk, oc) + 1)
                nc.vector.tensor_copy(k_hi[:, oc, cols], lin[:, NO + oc]).then_inc(k_hi_done, 1)
                dve.wait_ge(k_hi_done, results(b, blk, oc) + 1)
                nc.vector.tensor_tensor(k_lo[:, oc, cols], lin[:, NO + oc], k_hi[:, oc, cols].bitcast(F32),
                                        ALU.subtract).then_inc(k_split, 1)

            def v_parts(blk, u):
                m = blk * TPB + u
                return v_hl[:, bass.ds(m, 2), 0:TC], v_hl[:, bass.ds(m, 2), TC:2 * TC]

            def v_add(g, u):
                n = g * TPB + u
                dve.wait_ge(v_ready, n + 2)
                dve.wait_ge(v_split, START + n)
                nc.vector.tensor_tensor(v_tmp[:], ps[:, V_BANK + u:V_BANK + u + 2, 0:TC],
                                        v_bias[:].rearrange("p (a c) -> p a c", a=1).broadcast_to([P, 2, TC]), ALU.add)\
                    .then_inc(v_read, 2)

            def v_high(g, blk, u):
                dve.wait_ge(v_read, START + g * TPB + u + 2)
                nc.vector.tensor_scalar(v_parts(blk, u)[0], v_tmp[:], 0.0, None, ALU.max).then_inc(v_hi_done, 2)

            def v_low(g, blk, u):
                dve.wait_ge(v_hi_done, g * TPB + u + 2)
                hi, lo = v_parts(blk, u)
                nc.vector.scalar_tensor_tensor(out=lo, in0=v_tmp[:], scalar=0.0, in1=hi.bitcast(F32), op0=ALU.max,
                                               op1=ALU.subtract).then_inc(v_split, 2)

            def kv_block(b, blk, last):
                g = b * NBLK + blk
                k1_high(b, blk)
                if last:
                    q_low(b * NT, 0)
                    q_low(b * NT + 1, 1)
                v_add(g, 0)
                v_high(g, blk, 0)
                if not last:
                    x_low_half(b, blk + 1, 0)
                v_low(g, blk, 0)
                v_add(g, 2)
                if not last:
                    x_low_half(b, blk + 1, 1)
                v_high(g, blk, 2)
                v_low(g, blk, 2)
                split_k(b, blk, 0)
                split_k(b, blk, 1)

            def global_sum(b, pair, chunks):
                for c in chunks:
                    dve.wait_ge(e_done, START + (b * NPAIR + pair) * NC + c + 1)
                    nc.vector.scalar_tensor_tensor(out=e_img[:, c % 2], in0=e_img[:, c % 2], scalar=1.0,
                                                   in1=x_img[:, c, bass.ds(pair * PAIR, PAIR)], op0=ALU.mult,
                                                   op1=ALU.mult, accum_out=ex_part[:, c, bass.ds(pair, 1)])\
                        .then_inc(ex_done, 1)

            def piece_stats(b, blk, c):
                dve.wait_ge(piece_in, (b * NBLK + blk) * (16 * TPB) + 16 * c + 16)
                nc.vector.tensor_reduce(max_part[:, c, bass.ds(blk, 1)], x_res[:, 0], AX.X, ALU.max)
                nc.vector.bn_stats(bn_part[:, c, bass.ds(blk, 1)].rearrange("p a s -> p (a s)"), x_res[:, 0])\
                    .then_inc(piece_read, 1)

            def copy_scores(t, j):
                if j % 2 == 0:
                    dve.wait_ge(probs_ready, START + (t - 1) * NCH + j // 2 + 1)
                if j == 0:
                    dve.wait_ge(max_ready, START + t)
                dve.wait_ge(scores_ready, START + t * NJ + j + 1)
                nc.vector.tensor_scalar(scores[:, key_cols(j)], ps[:, S_BANK + j % RING_S], SCALE, None, ALU.mult,
                                        ALU.max, accum_out=blk_max[:, j:j + 1]).then_inc(scores_copied, 1)

            def row_max(t, parity):
                dve.wait_ge(scores_copied, START + t * NJ + NJ)
                nc.vector.tensor_reduce(neg_max[:, parity:parity + 1], blk_max[:], AX.X, ALU.max, negate=True)\
                    .then_inc(max_ready, 1)

            def pt_low(t, j):
                dve.wait_ge(pt_hi_done, t * NJ + j + 1)
                nc.vector.tensor_tensor(pt_lo[:, j % RING_PT], ps[:, T_BANK + j % RING_T],
                                        pt_hi[:, j % RING_PT].bitcast(F32), ALU.subtract).then_inc(pt_split, 1)

            def row_inverse(t, parity):
                dve.wait_ge(probs_ready, START + t * NCH + NCH)
                dve.wait_ge(inv_ready, START + t)
                nc.vector.tensor_reduce(row_sum[:], row_sums[:, parity], AX.X, ALU.add).then_inc(sum_done, 1)
                dve.wait_ge(sum_done, t + 1)
                dve.wait_ge(part_ready, START + t - 1)
                nc.vector.reciprocal(row_inv[:, parity:parity + 1], row_sum[:]).then_inc(inv_ready, 1)

            def finish_context(t, parity):
                dve.wait_ge(part_ready, START + t + 1)
                dve.wait_ge(ct_ready, START + t)
                nc.vector.scalar_tensor_tensor(out=ctx_row[:], in0=ps[:, CTX_BANK + parity, 0:TC],
                                               scalar=row_inv[:, parity:parity + 1], in1=ctx_part[:],
                                               op0=ALU.mult, op1=ALU.add).then_inc(ctx_ready, 1)

            def ct_low(t, i):
                dve.wait_ge(ct_hi_done, t + 1)
                nc.vector.tensor_tensor(ct_lo[:, :, i * P:(i + 1) * P],
                                        ps[:, CT_BANK, 0:TC].rearrange("p (o n) -> p o n", o=NO),
                                        ct_hi[:, :, i * P:(i + 1) * P].bitcast(F32), ALU.subtract).then_inc(ct_split, 1)

            def q_low(t, slot):
                dve.wait_ge(q_hi_done, t + 1)
                nc.vector.tensor_tensor(q_lo[:, slot], q_raw[:, slot], q_hi[:, slot].bitcast(F32), ALU.subtract)\
                    .then_inc(q_split, 1)

            def attend(b, blk, last, more_images):
                g = b * NBLK + blk
                for i in range(TPB):
                    t = g * TPB + i
                    more = not last or i < TPB - 1
                    own = i == TPB - 1
                    for j in range(NJ):
                        if more_images and j == 3:
                            piece_stats(b, blk, i)
                        if more and j < (HELD if own else NJ - 1):
                            copy_scores(t + 1, j)
                        pt_low(t, j)
                        if more and not own and j == NJ - 1:
                            copy_scores(t + 1, j)
                            row_max(t + 1, (i + 1) % 2)
                        if i > 0 and j == 2:
                            finish_context(t - 1, (i - 1) % 2)
                        if i > 0 and j == 4:
                            ct_low(t - 1, i - 1)
                        if j == 4:
                            row_inverse(t, i % 2)
                        if own and last and more_images and j == 3:
                            channel_means(b + 1, False)
                        if own and last and more_images and j == 5:
                            channel_variances(b + 1)
                        if own and last and more_images and j == 6:
                            group_variance(b + 1)
                        if j == 5 and (not last or i < TPB - 2):
                            q_low(t + 2, i % 2)
                    if own:
                        finish_context(t, i % 2)
                        if more:
                            copy_scores(t + 1, HELD)
                        ct_low(t, i)
                        if last and more_images:
                            coefficients(b + 1)
                            exp_bias(b + 1)
                            first_blocks(b + 1, lambda: None)
                        if more:
                            for j in range(HELD + 1, NJ):
                                copy_scores(t + 1, j)
                            row_max(t + 1, (i + 1) % 2)

            STAT_STEPS, GLOB_STEPS = 8, 6

            def stat(b, n, ins):
                ins.then_inc(stat_step, 1)
                dve.wait_ge(stat_step, b * STAT_STEPS + n)

            def glob(b, n, ins):
                ins.then_inc(glob_step, 1)
                dve.wait_ge(glob_step, b * GLOB_STEPS + n)

            def channel_means(b, first):
                if not first:
                    dve.wait_ge(piece_read, START + b * NT)
                    nc.vector.tensor_reduce(x_max[:], max_part[:], AX.X, ALU.max).then_inc(x_max_done, 1)
                for c in range(NC):
                    last = nc.vector.bn_aggr(mean_var[:, c], bn_part[:, c])
                stat(b, 1, last)
                nc.vector.tensor_copy(small[:, 2], mean_var[:, :, 0]).then_inc(stat_mean, 1)

            def channel_variances(b):
                dve.wait_ge(mean_ready, b + 1)
                stat(b, 2, nc.vector.tensor_copy(mean_g[:], ps[:, S_BANK, 0:NC]))
                stat(b, 3, nc.vector.tensor_tensor(small[:, 4], mean_var[:, :, 0], mean_g[:], ALU.subtract))
                stat(b, 4, nc.vector.tensor_tensor(small[:, 4], small[:, 4], small[:, 4], ALU.mult))
                nc.vector.tensor_tensor(small[:, 3], small[:, 4], mean_var[:, :, 1], ALU.add).then_inc(stat_var, 1)

            def group_variance(b):
                dve.wait_ge(var_ready, b + 1)
                nc.vector.tensor_scalar(small[:, 0], ps[:, S_BANK, 0:NC], EPS, None, ALU.add).then_inc(ve_ready, 1)

            def coefficients(b):
                dve.wait_ge(sqrt_done, b + 1)
                stat(b, 5, nc.vector.reciprocal(small[:, 4], small[:, 1]))
                stat(b, 6, nc.vector.tensor_tensor(small[:, 5], small[:, 4], small[:, 4], ALU.mult))
                stat(b, 7, nc.vector.tensor_tensor(small[:, 5], small[:, 5], small[:, 0], ALU.mult))
                stat(b, 8, nc.vector.tensor_scalar(small[:, 5], small[:, 5], -0.5, 1.5, ALU.mult, ALU.add))
                nc.vector.tensor_tensor(rstd[:], small[:, 4], small[:, 5], ALU.mult)
                nc.vector.tensor_scalar(neg_mean[:], mean_g[:], -1.0, None, ALU.mult).then_inc(coef_ready, 1)

            def image_block(n):
                return lambda c: x_img[:, c, bass.ds(n * BLK, BLK)]

            def first_blocks(b, between):
                dve.wait_ge(coef_ready, b + 1)
                dve.wait_ge(img_ready, b * NBLK + 1)
                x_normalise(b, 0, image_block(0))
                between()
                x_low_block(b, 0, x_hi, x_lo, HALVES)
                dve.wait_ge(img_ready, b * NBLK + 2)
                x_normalise(b, 1, image_block(1))
                between()
                x_low_block(b, 1, x_hi_odd, x_lo_odd)

            def exp_bias(b):
                dve.wait_ge(coef_ready, b + 1)
                dve.wait_ge(x_max_done, b + 1)
                nc.vector.scalar_tensor_tensor(out=e_bias[:], in0=x_max[:], scalar=-1.0, in1=rstd[:], op0=ALU.mult,
                                               op1=ALU.mult).then_inc(e_bias_ready, 1)

            def image(b, more_images):
                q1_high(b, 0)
                with dve.Fori(1, NPAIR) as pair:
                    n = pair * 2
                    dve.wait_ge(img_ready, b * NBLK + pair * 2 + 2)
                    x_normalise(b, n, image_block(n))
                    global_sum(b, pair - 1, (0, 1))
                    x_low_block(b, n, x_hi, x_lo)
                    q1_high(b, n - 1)
                    x_normalise(b, n + 1, image_block(n + 1))
                    global_sum(b, pair - 1, (2, 3))
                    x_low_block(b, n + 1, x_hi_odd, x_lo_odd)
                    q1_high(b, n)
                x_normalise(b, NBLK, image_block(0))
                global_sum(b, NPAIR - 1, (0, 1))
                x_low_block(b, NBLK, x_hi, x_lo)
                q1_high(b, NBLK - 1)
                q1_low(b, NBLK - 1)
                global_sum(b, NPAIR - 1, (2, 3))
                dve.wait_ge(ex_done, START + (b + 1) * (NPAIR * NC))
                nc.vector.tensor_reduce(e_sum[:], e_part[:], AX.X, ALU.add)
                glob(b, 1, nc.vector.tensor_reduce(ex_sum[:], ex_part[:], AX.X, ALU.add))
                glob(b, 2, nc.vector.reciprocal(small[:, 4], e_sum[:]))
                glob(b, 3, nc.vector.tensor_tensor(small[:, 4], small[:, 4], ex_sum[:], ALU.mult))
                glob(b, 4, nc.vector.tensor_tensor(small[:, 4], small[:, 4], mean_g[:], ALU.subtract))
                glob(b, 5, nc.vector.scalar_tensor_tensor(out=g_vec[:], in0=small[:, 4], scalar=1.0 / HW,
                                                          in1=rstd[:], op0=ALU.mult, op1=ALU.mult))
                for c in range(NC):
                    last = nc.vector.tensor_scalar(g_wide[:, c], group_mean[:], 0.0, g_vec[:, c:c + 1], ALU.mult,
                                                   ALU.add)
                last.then_inc(g_ready, 1)
                dve.wait_ge(glob_ready, b + 1)
                nc.vector.tensor_tensor(k_bias[:], ps[:, 7, 8:8 + NO], aff[:, KG1:KG1 + NO], ALU.mult)
                glob(b, 6, nc.vector.tensor_tensor(v_bias[:], ps[:, 6, 0:TC], vaff[:, 0], ALU.mult))
                nc.vector.tensor_tensor(k_bias[:], k_bias[:], aff[:, KB1:KB1 + NO], ALU.add)
                nc.vector.tensor_tensor(v_bias[:], v_bias[:], vaff[:, 1], ALU.add).then_inc(glob_done, 1)
                dve.wait_ge(glob_done, b + 1)
                with dve.Fori(0, NBLK - 1) as blk:
                    kv_block(b, blk, False)
                kv_block(b, NBLK - 1, True)
                for j in range(NJ):
                    copy_scores(b * NT, j)
                row_max(b * NT, 0)
                with dve.Fori(0, NBLK - 1) as blk:
                    attend(b, blk, False, more_images)
                attend(b, NBLK - 1, True, more_images)

            maxima = iter(range(NBLK))

            def next_max():
                n = next(maxima)
                nc.vector.tensor_reduce(max_part[:, :, n], x_img[:, :, key_cols(n)], AX.X, ALU.max)\
                    .then_inc(first_max, 1)

            for n in range(NBLK):
                dve.wait_ge(img_ready, n + 1)
                for c in range(NC):
                    last = nc.vector.bn_stats(bn_part[:, c, n], x_img[:, c, key_cols(n)])
                if n in (2, 5):
                    next_max()
            last.then_inc(first_stats, 1)
            next_max()
            dve.wait_ge(first_stats, 1)
            channel_means(0, True)
            dve.wait_ge(const_in, 64)
            next_max()
            channel_variances(0)
            next_max()
            group_variance(0)
            coefficients(0)
            first_blocks(0, next_max)
            next_max()
            dve.wait_ge(first_max, NBLK)
            nc.vector.tensor_reduce(x_max[:], max_part[:], AX.X, ALU.max).then_inc(x_max_done, 1)
            exp_bias(0)
            with dve.Fori(0, BATCH - 1) as b:
                image(b, True)
            image(BATCH - 1, False)


def kernel(**inputs):
    import numpy as np
    import concourse.bacc as bacc
    from concourse.bass_utils import run_bass_kernel_spmd as run

    a = {k.replace("L0_conv_", ""): np.asarray(v) for k, v in inputs.items()}

    def per_channel(v):
        return v.reshape(-1, P).T

    k_t, v_t = a["k_w1"].T, a["v_w"].T
    w_proj = np.concatenate([a["q_w1"].T, a["q_w2"].T, k_t[C:], v_t[C:], a["k_w2"].T], 0)
    w_glob = np.concatenate([k_t[:C], v_t[:C]], 0)
    affine = np.concatenate([per_channel(a[n]) for n in
                             ("q_g1", "q_b1", "q_g2", "q_b2", "k_g1", "k_b1", "k_g2", "k_b2", "o_g", "o_b")], 1)
    v_affine = np.stack([np.repeat(a["v_g"][None], P, 0), np.repeat(a["v_b"][None], P, 0)], 1)
    channel = np.arange(P)
    same_group = channel[:, None] // GROUP == channel[None] // GROUP
    arrays = {
        "x": a["x"].reshape(BATCH, NC, P, HW),
        "w_proj": w_proj,
        "w_glob": w_glob,
        "w_out": a["o_w"].T,
        "affine": affine,
        "v_affine": v_affine,
        "ident": np.eye(P, dtype=np.float32),
        "group": np.where(same_group, 1.0 / GROUP, 0.0).astype(np.float32),
    }
    arrays = {f"in_{k}_dram": np.ascontiguousarray(v) for k, v in arrays.items()}
    nc = bacc.Bacc("TRN2", target_bir_lowering=False, num_devices=1)
    args = [nc.dram_tensor(k, v.shape, F32, kind="ExternalInput").ap() for k, v in arrays.items()]
    out = nc.dram_tensor("out_0_dram", (BATCH, NC, P, HW), F32, kind="ExternalOutput").ap()
    build(nc, *args, out)
    r = run(nc, [arrays], core_ids=[0])
    return r.results[0]["out_0_dram"].reshape(BATCH, C, 64, 64)
```
